# Optimizing a Trainium2 kernel written in Bass

```python
import numpy as np
import jax
import jax.numpy as jnp

def _softmax(x, axis=-1):
    return jax.nn.softmax(x, axis=axis)

def _gelu(x):
    return jax.nn.gelu(x, approximate=True)

def _silu(x):
    return jax.nn.silu(x)

def _sigmoid(x):
    return jax.nn.sigmoid(x)

def _layernorm(x, axis=-1, eps=1e-05):
    m = jnp.mean(x, axis=axis, keepdims=True)
    v = jnp.var(x, axis=axis, keepdims=True)
    return (x - m) / jnp.sqrt(v + eps)

def _scatter_add(tgt, idx, src, axis=0):
    return tgt.at[idx].add(src)

def _segment_sum(src, seg, n):
    return jax.ops.segment_sum(src, seg, n)
kernel_name = 'mk_adaln_d2_jaxref_r8_f249de'

def setup_inputs(seed: int=0):
    np.random.seed(seed)
    _w = jnp.asarray

    def _L0_attn_setup():
        import jax, jax.numpy as jnp
        import numpy as np
        B, S, D_IN, D_H = (8, 256, 128, 128)
        LR = 0.01
        key = jax.random.key(seed)
        ks = jax.random.split(key, 6)
        return {'in_seq': jax.random.normal(ks[0], (B, S, D_IN), jnp.float32), 'theta_K': jax.random.normal(ks[1], (D_H, D_IN), jnp.float32) * 0.02, 'theta_V': jax.random.normal(ks[2], (D_H, D_IN), jnp.float32) * 0.02, 'theta_Q': jax.random.normal(ks[3], (D_H, D_IN), jnp.float32) * 0.02, 'W0': jax.random.normal(ks[4], (D_H, D_H), jnp.float32) * 0.02, 'b0': jnp.zeros((D_H,), jnp.float32)}
    _L0_attn_in = _L0_attn_setup()

    def _L0_ffn_setup():
        import jax, jax.numpy as jnp
        import numpy as np
        DIM = 128
        DEPTH = 6
        HEADS = 16
        DIM_HEAD = 64
        WINDOW = 32
        INNER = HEADS * DIM_HEAD
        DIM_INNER = int(DIM * 4 * 2 / 3)
        QK_SCALE = 8.0

        def shift_tokens(t):
            a, s = jnp.split(t, 2, -1)
            s = jnp.pad(s, ((0, 0), (1, 0), (0, 0)))[:, :-1]
            return jnp.concatenate([a, s], -1)

        def l2norm(t):
            return t / jnp.maximum(jnp.linalg.norm(t, axis=-1, keepdims=True), 1e-12)

        def rotate_half(x):
            x1, x2 = jnp.split(x, 2, -1)
            return jnp.concatenate([-x2, x1], -1)

        def rotary_tables(n):
            half = jnp.arange(0, DIM_HEAD, 2, dtype=jnp.float32)
            inv_freq = 1.0 / 10000.0 ** (half / DIM_HEAD)
            t = jnp.arange(n, dtype=jnp.float32)
            freqs = t[:, None] * inv_freq[None, :]
            freqs = jnp.concatenate([freqs, freqs], -1)
            base_scale = (half + 0.4 * DIM_HEAD) / (1.4 * DIM_HEAD)
            power = (t - n // 2) / (WINDOW // 2)
            scale = base_scale[None, :] ** power[:, None]
            scale = jnp.concatenate([scale, scale], -1)
            return (freqs, scale)

        def local_attention(q, k, v):
            b, h, n, d = q.shape
            w = WINDOW
            nw = n // w
            bq = q.reshape(b, h, nw, w, d)
            bk = k.reshape(b, h, nw, w, d)
            bv = v.reshape(b, h, nw, w, d)

            def look(t):
                p = jnp.pad(t, ((0, 0), (0, 0), (1, 0), (0, 0), (0, 0)))
                return jnp.concatenate([p[:, :, :nw], p[:, :, 1:]], axis=3)
            bk2, bv2 = (look(bk), look(bv))
            seq = jnp.arange(n).reshape(nw, w)
            seq_p = jnp.pad(seq, ((1, 0), (0, 0)), constant_values=-1)
            jt = jnp.concatenate([seq_p[:nw], seq_p[1:]], axis=1)
            it = seq[:, :, None]
            jb = jt[:, None, :]
            mask = (it < jb) | (it > jb + w) | (jb == -1)
            sim = jnp.einsum('bhwie,bhwje->bhwij', bq, bk2) * QK_SCALE
            sim = jnp.where(mask, -jnp.finfo(sim.dtype).max, sim)
            attn = jax.nn.softmax(sim, -1)
            out = jnp.einsum('bhwij,bhwje->bhwie', attn, bv2)
            return out.reshape(b, h, n, d)

        def attn_layer(x, Wqkv, qs, ksc, Wo):
            b, n, _ = x.shape
            qkv = x @ Wqkv
            q, k, v = jnp.split(qkv, 3, -1)
            sh = lambda t: t.reshape(b, n, HEADS, DIM_HEAD).transpose(0, 2, 1, 3)
            q, k, v = (sh(q), sh(k), sh(v))
            q = l2norm(q) * qs
            k = l2norm(k) * ksc
            freqs, scale = rotary_tables(n)
            cos, sin = (jnp.cos(freqs), jnp.sin(freqs))
            q = q * cos * scale + rotate_half(q) * sin * scale
            inv = 1.0 / scale
            k = k * cos * inv + rotate_half(k) * sin * inv
            out = local_attention(q, k, v)
            out = out.transpose(0, 2, 1, 3).reshape(b, n, INNER)
            return out @ Wo

        def ffn_layer(x, g, bln, W1, b1, W2, b2):
            mu = x.mean(-1, keepdims=True)
            var = ((x - mu) ** 2).mean(-1, keepdims=True)
            xn = (x - mu) / jnp.sqrt(var + 1e-05) * g + bln
            hg = xn @ W1 + b1
            a, gate = jnp.split(hg, 2, -1)
            return a * jax.nn.gelu(gate, approximate=False) @ W2 + b2
        key = jax.random.key(seed)
        ks = jax.random.split(key, 8)
        B, N = (2, 256)
        init = lambda k, shape: jax.random.normal(k, shape, jnp.float32) * 0.02
        return {'x': jax.random.normal(ks[0], (B, N, DIM), jnp.float32), 'Wqkv': init(ks[1], (DEPTH, DIM, 3 * INNER)), 'q_scale': jnp.ones((DEPTH, DIM_HEAD), jnp.float32), 'k_scale': jnp.ones((DEPTH, DIM_HEAD), jnp.float32), 'Wo': init(ks[2], (DEPTH, INNER, DIM)), 'ln_g': jnp.ones((DEPTH, DIM), jnp.float32), 'ln_b': jnp.zeros((DEPTH, DIM), jnp.float32), 'W1': init(ks[3], (DEPTH, DIM, 2 * DIM_INNER)), 'b1': jnp.zeros((DEPTH, 2 * DIM_INNER), jnp.float32), 'W2': init(ks[4], (DEPTH, DIM_INNER, DIM)), 'b2': jnp.zeros((DEPTH, DIM), jnp.float32)}
    _L0_ffn_in = _L0_ffn_setup()
    _L0_c = _w((lambda *s: np.random.randn(*s).astype(np.float32) * 0.05)(4, 128))
    _L0_wmod = _w((lambda *s: np.random.randn(*s).astype(np.float32) * 0.05)(128, 6 * 128) * 128 ** (-0.5))

    def _L1_attn_setup():
        import jax, jax.numpy as jnp
        import numpy as np
        NUM_HEADS = 16
        key = jax.random.key(seed)
        ks = jax.random.split(key, 11)
        B, S, D = (4, 128, 128)
        M = 128
        hd = D // NUM_HEADS
        s = 0.02
        return {'x': jax.random.normal(ks[0], (B, S, D), jnp.float32), 'Wq': jax.random.normal(ks[1], (D, D), jnp.float32) * s, 'bq': jax.random.normal(ks[2], (D,), jnp.float32) * s, 'Wk': jax.random.normal(ks[3], (D, D), jnp.float32) * s, 'bk': jax.random.normal(ks[4], (D,), jnp.float32) * s, 'Wv': jax.random.normal(ks[5], (D, D), jnp.float32) * s, 'bv': jax.random.normal(ks[6], (D,), jnp.float32) * s, 'Wo': jax.random.normal(ks[7], (D, D), jnp.float32) * s, 'bo': jax.random.normal(ks[8], (D,), jnp.float32) * s, 'rel_k': jax.random.normal(ks[9], (2 * M + 1, hd), jnp.float32), 'rel_v': jax.random.normal(ks[10], (2 * M + 1, hd), jnp.float32)}
    _L1_attn_in = _L1_attn_setup()

    def _L1_ffn_setup():
        import jax, jax.numpy as jnp
        import numpy as np
        B, T, D, E = (4, 128, 128, 8)
        HD = 4 * D
        key = jax.random.key(seed)
        k1, k2, k3, k4 = jax.random.split(key, 4)
        std = 0.5 * D ** (-0.5)
        bound = 3.0 ** 0.5 * std
        x = jax.random.normal(k1, (B, T, D), dtype=jnp.float32)
        router_w = jax.random.normal(k2, (E, D), dtype=jnp.float32) * 0.02
        expert_fc = jax.random.uniform(k3, (E, D, HD), dtype=jnp.float32, minval=-bound, maxval=bound)
        expert_proj = jax.random.normal(k4, (E, D, HD), dtype=jnp.float32) * 0.02
        return {'x': x, 'router_w': router_w, 'expert_fc': expert_fc, 'expert_proj': expert_proj}
    _L1_ffn_in = _L1_ffn_setup()
    _L1_c = _w((lambda *s: np.random.randn(*s).astype(np.float32) * 0.05)(4, 128))
    _L1_wmod = _w((lambda *s: np.random.randn(*s).astype(np.float32) * 0.05)(128, 6 * 128) * 128 ** (-0.5))
    _d = {'L0_attn_in_seq': _L0_attn_in['in_seq'], 'L0_attn_theta_K': _L0_attn_in['theta_K'], 'L0_attn_theta_V': _L0_attn_in['theta_V'], 'L0_attn_theta_Q': _L0_attn_in['theta_Q'], 'L0_attn_W0': _L0_attn_in['W0'], 'L0_attn_b0': _L0_attn_in['b0'], 'L0_ffn_Wqkv': _L0_ffn_in['Wqkv'], 'L0_ffn_q_scale': _L0_ffn_in['q_scale'], 'L0_ffn_k_scale': _L0_ffn_in['k_scale'], 'L0_ffn_Wo': _L0_ffn_in['Wo'], 'L0_ffn_ln_g': _L0_ffn_in['ln_g'], 'L0_ffn_ln_b': _L0_ffn_in['ln_b'], 'L0_ffn_W1': _L0_ffn_in['W1'], 'L0_ffn_b1': _L0_ffn_in['b1'], 'L0_ffn_W2': _L0_ffn_in['W2'], 'L0_ffn_b2': _L0_ffn_in['b2'], 'L0_c': _L0_c, 'L0_wmod': _L0_wmod, 'L1_attn_Wq': _L1_attn_in['Wq'], 'L1_attn_bq': _L1_attn_in['bq'], 'L1_attn_Wk': _L1_attn_in['Wk'], 'L1_attn_bk': _L1_attn_in['bk'], 'L1_attn_Wv': _L1_attn_in['Wv'], 'L1_attn_bv': _L1_attn_in['bv'], 'L1_attn_Wo': _L1_attn_in['Wo'], 'L1_attn_bo': _L1_attn_in['bo'], 'L1_attn_rel_k': _L1_attn_in['rel_k'], 'L1_attn_rel_v': _L1_attn_in['rel_v'], 'L1_ffn_router_w': _L1_ffn_in['router_w'], 'L1_ffn_expert_fc': _L1_ffn_in['expert_fc'], 'L1_ffn_expert_proj': _L1_ffn_in['expert_proj'], 'L1_c': _L1_c, 'L1_wmod': _L1_wmod}
    _x0 = _d['L0_attn_in_seq']
    _d['L0_attn_in_seq'] = jax.random.normal(jax.random.fold_in(jax.random.key(seed), 1), (4, 512, 128), dtype=_x0.dtype)
    del _x0
    return _d

def reference(L0_attn_in_seq, L0_attn_theta_K, L0_attn_theta_V, L0_attn_theta_Q, L0_attn_W0, L0_attn_b0, L0_ffn_Wqkv, L0_ffn_q_scale, L0_ffn_k_scale, L0_ffn_Wo, L0_ffn_ln_g, L0_ffn_ln_b, L0_ffn_W1, L0_ffn_b1, L0_ffn_W2, L0_ffn_b2, L0_c, L0_wmod, L1_attn_Wq, L1_attn_bq, L1_attn_Wk, L1_attn_bk, L1_attn_Wv, L1_attn_bv, L1_attn_Wo, L1_attn_bo, L1_attn_rel_k, L1_attn_rel_v, L1_ffn_router_w, L1_ffn_expert_fc, L1_ffn_expert_proj, L1_c, L1_wmod):

    def _L0_attn_ref(in_seq, theta_K, theta_V, theta_Q, W0, b0):
        import jax, jax.numpy as jnp
        import numpy as np
        B, S, D_IN, D_H = (8, 256, 128, 128)
        LR = 0.01
        'TTT layer: per-token inner SGD step on MSE(W@k+b, v), then predict W@q+b.'
        d_h = W0.shape[0]
        K = jnp.einsum('bsd,ed->bse', in_seq, theta_K)
        V = jnp.einsum('bsd,ed->bse', in_seq, theta_V)
        Q = jnp.einsum('bsd,ed->bse', in_seq, theta_Q)

        def step(carry, kvq):
            W, b = carry
            k, v, q = kvq
            pred = W @ k + b
            g = 2.0 / d_h * (pred - v)
            W = W - LR * jnp.outer(g, k)
            b = b - LR * g
            out = W @ q + b
            return ((W, b), out)

        def run_seq(k_s, v_s, q_s):
            _, ys = jax.lax.scan(step, (W0, b0), (k_s, v_s, q_s))
            return ys
        return jax.vmap(run_seq)(K, V, Q)

    def _L0_ffn_ref(x, Wqkv, q_scale, k_scale, Wo, ln_g, ln_b, W1, b1, W2, b2):
        import jax, jax.numpy as jnp
        import numpy as np
        DIM = 128
        DEPTH = 6
        HEADS = 16
        DIM_HEAD = 64
        WINDOW = 32
        INNER = HEADS * DIM_HEAD
        DIM_INNER = int(DIM * 4 * 2 / 3)
        QK_SCALE = 8.0

        def shift_tokens(t):
            a, s = jnp.split(t, 2, -1)
            s = jnp.pad(s, ((0, 0), (1, 0), (0, 0)))[:, :-1]
            return jnp.concatenate([a, s], -1)

        def l2norm(t):
            return t / jnp.maximum(jnp.linalg.norm(t, axis=-1, keepdims=True), 1e-12)

        def rotate_half(x):
            x1, x2 = jnp.split(x, 2, -1)
            return jnp.concatenate([-x2, x1], -1)

        def rotary_tables(n):
            half = jnp.arange(0, DIM_HEAD, 2, dtype=jnp.float32)
            inv_freq = 1.0 / 10000.0 ** (half / DIM_HEAD)
            t = jnp.arange(n, dtype=jnp.float32)
            freqs = t[:, None] * inv_freq[None, :]
            freqs = jnp.concatenate([freqs, freqs], -1)
            base_scale = (half + 0.4 * DIM_HEAD) / (1.4 * DIM_HEAD)
            power = (t - n // 2) / (WINDOW // 2)
            scale = base_scale[None, :] ** power[:, None]
            scale = jnp.concatenate([scale, scale], -1)
            return (freqs, scale)

        def local_attention(q, k, v):
            b, h, n, d = q.shape
            w = WINDOW
            nw = n // w
            bq = q.reshape(b, h, nw, w, d)
            bk = k.reshape(b, h, nw, w, d)
            bv = v.reshape(b, h, nw, w, d)

            def look(t):
                p = jnp.pad(t, ((0, 0), (0, 0), (1, 0), (0, 0), (0, 0)))
                return jnp.concatenate([p[:, :, :nw], p[:, :, 1:]], axis=3)
            bk2, bv2 = (look(bk), look(bv))
            seq = jnp.arange(n).reshape(nw, w)
            seq_p = jnp.pad(seq, ((1, 0), (0, 0)), constant_values=-1)
            jt = jnp.concatenate([seq_p[:nw], seq_p[1:]], axis=1)
            it = seq[:, :, None]
            jb = jt[:, None, :]
            mask = (it < jb) | (it > jb + w) | (jb == -1)
            sim = jnp.einsum('bhwie,bhwje->bhwij', bq, bk2) * QK_SCALE
            sim = jnp.where(mask, -jnp.finfo(sim.dtype).max, sim)
            attn = jax.nn.softmax(sim, -1)
            out = jnp.einsum('bhwij,bhwje->bhwie', attn, bv2)
            return out.reshape(b, h, n, d)

        def attn_layer(x, Wqkv, qs, ksc, Wo):
            b, n, _ = x.shape
            qkv = x @ Wqkv
            q, k, v = jnp.split(qkv, 3, -1)
            sh = lambda t: t.reshape(b, n, HEADS, DIM_HEAD).transpose(0, 2, 1, 3)
            q, k, v = (sh(q), sh(k), sh(v))
            q = l2norm(q) * qs
            k = l2norm(k) * ksc
            freqs, scale = rotary_tables(n)
            cos, sin = (jnp.cos(freqs), jnp.sin(freqs))
            q = q * cos * scale + rotate_half(q) * sin * scale
            inv = 1.0 / scale
            k = k * cos * inv + rotate_half(k) * sin * inv
            out = local_attention(q, k, v)
            out = out.transpose(0, 2, 1, 3).reshape(b, n, INNER)
            return out @ Wo

        def ffn_layer(x, g, bln, W1, b1, W2, b2):
            mu = x.mean(-1, keepdims=True)
            var = ((x - mu) ** 2).mean(-1, keepdims=True)
            xn = (x - mu) / jnp.sqrt(var + 1e-05) * g + bln
            hg = xn @ W1 + b1
            a, gate = jnp.split(hg, 2, -1)
            return a * jax.nn.gelu(gate, approximate=False) @ W2 + b2
        for i in range(DEPTH):
            x = attn_layer(shift_tokens(x), Wqkv[i], q_scale[i], k_scale[i], Wo[i]) + x
            x = ffn_layer(shift_tokens(x), ln_g[i], ln_b[i], W1[i], b1[i], W2[i], b2[i]) + x
        return x

    def _L1_attn_ref(x, Wq, bq, Wk, bk, Wv, bv, Wo, bo, rel_k, rel_v):
        import jax, jax.numpy as jnp
        import numpy as np
        NUM_HEADS = 16
        B, S, D = x.shape
        H = NUM_HEADS
        hd = D // H
        M = (rel_k.shape[0] - 1) // 2

        def proj(W, b):
            return (x @ W.T + b).reshape(B, S, H, hd).transpose(0, 2, 1, 3)
        q = proj(Wq, bq)
        k = proj(Wk, bk)
        v = proj(Wv, bv)
        r = jnp.arange(S)
        idx = jnp.clip(r[None, :] - r[:, None], -M, M) + M
        rpk = rel_k[idx]
        rpv = rel_v[idx]
        content = jnp.einsum('bhqd,bhkd->bhqk', q, k)
        relative = jnp.einsum('bhqd,qkd->bhqk', q, rpk)
        scores = (content + relative) / jnp.sqrt(jnp.float32(hd))
        w = jax.nn.softmax(scores, axis=-1)
        out = jnp.einsum('bhqk,bhkd->bhqd', w, v) + jnp.einsum('bhqk,qkd->bhqd', w, rpv)
        out = out.transpose(0, 2, 1, 3).reshape(B, S, D)
        return out @ Wo.T + bo

    def _L1_ffn_ref(x, router_w, expert_fc, expert_proj):
        import jax, jax.numpy as jnp
        import numpy as np
        B, T, D, E = (4, 128, 128, 8)
        HD = 4 * D
        logits = jnp.einsum('btd,ed->bte', x, router_w)
        probs = jax.nn.softmax(logits, axis=-1)
        expert_ids = jnp.argmax(probs, axis=-1)
        mask = jax.nn.one_hot(expert_ids, E, dtype=x.dtype)
        h = jnp.einsum('btd,edh->ebth', x, expert_fc)
        h = jnp.square(jax.nn.relu(h))
        out_e = jnp.einsum('ebth,edh->ebtd', h, expert_proj)
        output = jnp.einsum('ebtd,bte->btd', out_e, mask)
        return output
    x = L0_attn_in_seq
    mod = (_silu(L0_c) @ L0_wmod).reshape(L0_c.shape[0], 6, 1, -1)
    sa, ca, ga, sb, cb, gb = (mod[:, 0], mod[:, 1], mod[:, 2], mod[:, 3], mod[:, 4], mod[:, 5])
    ga = (2 * (ga >= 0) - 1) * jnp.maximum(jnp.abs(ga), 0.25)
    gb = (2 * (gb >= 0) - 1) * jnp.maximum(jnp.abs(gb), 0.25)
    h = _layernorm(x, axis=-1) * (1 + ca) + sa
    x = x + ga * _L0_attn_ref(h, L0_attn_theta_K, L0_attn_theta_V, L0_attn_theta_Q, L0_attn_W0, L0_attn_b0)
    h = _layernorm(x, axis=-1) * (1 + cb) + sb
    x = x + gb * _L0_ffn_ref(h, L0_ffn_Wqkv, L0_ffn_q_scale, L0_ffn_k_scale, L0_ffn_Wo, L0_ffn_ln_g, L0_ffn_ln_b, L0_ffn_W1, L0_ffn_b1, L0_ffn_W2, L0_ffn_b2)
    mod = (_silu(L1_c) @ L1_wmod).reshape(L1_c.shape[0], 6, 1, -1)
    sa, ca, ga, sb, cb, gb = (mod[:, 0], mod[:, 1], mod[:, 2], mod[:, 3], mod[:, 4], mod[:, 5])
    ga = (2 * (ga >= 0) - 1) * jnp.maximum(jnp.abs(ga), 0.25)
    gb = (2 * (gb >= 0) - 1) * jnp.maximum(jnp.abs(gb), 0.25)
    h = _layernorm(x, axis=-1) * (1 + ca) + sa
    x = x + ga * _L1_attn_ref(h, L1_attn_Wq, L1_attn_bq, L1_attn_Wk, L1_attn_bk, L1_attn_Wv, L1_attn_bv, L1_attn_Wo, L1_attn_bo, L1_attn_rel_k, L1_attn_rel_v)
    h = _layernorm(x, axis=-1) * (1 + cb) + sb
    x = x + gb * _L1_ffn_ref(h, L1_ffn_router_w, L1_ffn_expert_fc, L1_ffn_expert_proj)
    return x

_drawn_inputs = setup_inputs


def setup_inputs(seed=0):
    import zlib

    import numpy as np

    out = dict(_drawn_inputs(seed))
    spreads = {'L0_attn_b0': (0.0, 0.349),
     'L0_ffn_q_scale': (1.0, 0.6),
     'L0_ffn_k_scale': (1.0, 0.6),
     'L0_ffn_ln_g': (1.0, 0.6),
     'L0_ffn_ln_b': (0.0, 0.8),
     'L0_ffn_b1': (0.0, 0.8),
     'L0_ffn_b2': (0.0, 0.53)}
    factors = {'L0_attn_theta_K': 8.0,
     'L0_attn_theta_V': 8.0,
     'L0_attn_theta_Q': 4.148,
     'L0_attn_W0': 4.226,
     'L0_ffn_W1': 6.894,
     'L0_ffn_W2': 6.653,
     'L1_attn_Wq': 37.607,
     'L1_attn_bq': 64.0,
     'L1_attn_Wk': 64.0,
     'L1_attn_bk': 64.0,
     'L1_attn_Wv': 38.607,
     'L1_attn_bv': 64.0,
     'L1_attn_bo': 64.0,
     'L1_attn_rel_k': 37.95,
     'L1_attn_Wo': 4.103,
     'L1_attn_rel_v': 8.0,
     'L1_ffn_router_w': 8.0,
     'L1_ffn_expert_fc': 8.0,
     'L1_ffn_expert_proj': 8.0,
     'L1_c': 3.811,
     'L1_wmod': 3.737}
    for name, (base, spread) in spreads.items():
        noise = np.random.default_rng([zlib.crc32(name.encode()), seed]).standard_normal(out[name].shape)
        drawn = base * np.exp(spread * noise) if base else spread * noise
        out[name] = jnp.asarray(drawn.astype(out[name].dtype))
    for name, factor in factors.items():
        out[name] = (out[name] * factor).astype(out[name].dtype)
    return out
```

```python
from contextlib import ExitStack

import numpy as np

import concourse.bass as bass
from concourse import mybir

F32 = mybir.dt.float32
BF16 = mybir.dt.bfloat16
I32 = mybir.dt.int32
ALU = mybir.AluOpType
ACT = mybir.ActivationFunctionType
AX = mybir.AxisListType.X

P = 128
B, S = 4, 512
NT = B * S // P
TPB = S // P
LN_EPS = 1e-5
ETA = 0.01 * 2.0 / P
DEPTH, HEADS, DH, WIN = 6, 16, 64, 32
INNER = HEADS * DH
PAIRS = HEADS // 2
QB = 64
KB = QB + WIN
GH = 4
DI = int(P * 4 * 2 / 3)
CHUNKS = [(0, 128), (128, 128), (256, DI - 256)]
MASKED = -1e30
H2 = 16
D2 = P // H2
M2 = 128
EXT = 2 * 2 * M2 - 1
ROW = 512
SPLITS = [(a, b) for a in range(3) for b in range(3)]
KS = len(SPLITS) * D2
NE, HD = 8, 512


class Engine:

    def __init__(self, nc, engine, name):
        self.e, self.name, self.sem = engine, name, nc.alloc_semaphore(name + "_done")
        self.count, self.seen = 0, {}

    def wait(self, *marks):
        for sem, value, name in [m for m in marks if m is not None]:
            if self.seen.get(name, 0) < value:
                self.e.wait_ge(sem, value)
                self.seen[name] = value

    def did(self, instruction):
        self.count += 1
        instruction.then_inc(self.sem, 1)
        return (self.sem, self.count, self.name)

    def last(self):
        return (self.sem, self.count, self.name) if self.count else None


class Loads:

    def __init__(self, nc, name):
        self.name, self.sem, self.count = name, nc.alloc_semaphore(name), 0

    def start(self, engine, out, in_):
        self.count += 16
        engine.e.dma_start(out, in_).then_inc(self.sem, 16)
        return self.mark()

    def mark(self):
        return (self.sem, self.count, self.name)


class Ring:

    def __init__(self, buffers):
        self.buffers, self.users, self.idle = buffers, [()] * len(buffers), list(range(len(buffers)))

    def take(self, *writers):
        i = self.idle.pop(0)
        for w in writers:
            w.wait(*self.users[i])
        return i, self.buffers[i]

    def done(self, i, *marks):
        assert i not in self.idle
        self.users[i] = marks
        self.idle.append(i)


class Core:
    pass


def build(nc, io, stop=99):
    with ExitStack() as whole:
        whole.enter_context(nc.allow_non_contiguous_dma(reason="small vectors loaded as columns"))
        build_body(nc, io, whole, stop)


def build_body(nc, io, whole, stop):
    PE, V = Engine(nc, nc.tensor, "pe"), Engine(nc, nc.vector, "dve")
    A, G = Engine(nc, nc.scalar, "act"), Engine(nc, nc.gpsimd, "pool")
    SP = Engine(nc, nc.sync, "sp")
    compute = (PE, V, A, G)

    def sbuf(stack, name, shape, dt=F32):
        return stack.enter_context(nc.sbuf_tensor(name, shape, dt))

    def scratch(name, shape, dt=F32):
        return nc.dram_tensor(name, shape, dt, kind="Internal").ap()

    psum = whole.enter_context(nc.psum_tensor("psum", [P, 8, 512], F32))
    banks = Ring([psum[:, i, :] for i in range(8)])

    def meet():
        marks = [x.last() for x in compute]
        for x in (*compute, SP):
            x.wait(*marks)

    ident = sbuf(whole, "ident", [P, P])
    identb = sbuf(whole, "identb", [P, P], BF16)
    center = sbuf(whole, "center", [P, P])
    ones = sbuf(whole, "ones", [P, P])
    xT = sbuf(whole, "xT", [P, B, S])
    modT = sbuf(whole, "modT", [P, 2, 6, B])
    gate = sbuf(whole, "gate", [P, 2, 2, B])
    rstd_tmp = sbuf(whole, "rstd_tmp", [P, 64])
    rstd = sbuf(whole, "rstd", [P, 2, 32])
    rstd_in = sbuf(whole, "rstd_in", [P, 2, 32])
    sq_ring = Ring([sbuf(whole, f"sq{i}", [P, 512]) for i in range(2)])

    first = Loads(nc, "first_loads")
    for dst, src in ((ident, "c_ident"), (center, "c_center")):
        first.start(SP, dst[:, :], io[src])
    o1 = V.did(V.e.memset(ones[:, :], 1.0))

    def inverse_root(y, x, t, x_mark, eng):
        V.wait(x_mark)
        m = V.did(V.e.tensor_scalar(t.bitcast(I32), x.bitcast(I32), 1, None, ALU.logical_shift_right))
        V.wait(m)
        m = V.did(V.e.tensor_scalar(y.bitcast(I32), t.bitcast(I32), -1.0, float(0x5F3759DF), ALU.mult, ALU.add))
        for _ in range(3):
            for out, a, b in ((t, y, y), (t, t, x), (t, t, None), (y, y, t)):
                eng.wait(m)
                if b is None:
                    m = eng.did(eng.e.tensor_scalar(out, a, -0.5, 1.5, ALU.mult, ALU.add))
                else:
                    m = eng.did(eng.e.tensor_tensor(out, a, b, ALU.mult))
        return m

    rstd_users = [(), ()]

    def layer_norm(dst, src, xc, scale, shift, k, *src_marks):
        k %= 2
        PE.wait(*src_marks)
        i, ps = banks.take(PE)
        m = PE.did(PE.e.matmul(ps, center[:, :], src, start=True, stop=True))
        si, sq = sq_ring.take(A)
        A.wait(m)
        A.did(A.e.activation(xc, ps, ACT.Copy))
        m = A.did(A.e.activation(sq[:, :], ps, ACT.Square))
        banks.done(i, m)
        xc_mark = m
        i, ps = banks.take(PE)
        PE.wait(m)
        for c in range(TPB):
            last = PE.e.matmul(ps[:, c:c + 1], sq[:, c * P:(c + 1) * P], ones[:, 0:1], start=True, stop=True)
        m = PE.did(last)
        sq_ring.done(si, m)
        var, r = rstd_in[:, k, 0:TPB], rstd[:, k, 0:TPB]
        V.wait(m, *rstd_users[k])
        m = V.did(V.e.tensor_scalar(var, ps[:, 0:TPB], 1.0 / P, LN_EPS, ALU.mult, ALU.add))
        banks.done(i, m)
        m = inverse_root(r, var, rstd_tmp[:, k * 8:k * 8 + TPB], m, V)
        i, ps = banks.take(PE)
        PE.wait(m)
        for c in range(TPB):
            last = PE.e.matmul(ps[:, c * P:(c + 1) * P], r[:, c:c + 1].to_broadcast([P, P]), ident[:, :], start=True, stop=True)
        m = PE.did(last)
        rstd_users[k] = (m,)
        V.wait(m, xc_mark)
        m = V.did(V.e.tensor_tensor(xc, xc, ps, ALU.mult))
        banks.done(i, m)
        V.wait(m)
        return V.did(V.e.tensor_scalar(dst, xc, scale, shift, ALU.mult, ALU.add))

    core = Core()
    core.nc = nc
    core.io = io
    core.PE = PE
    core.V = V
    core.A = A
    core.G = G
    core.SP = SP
    core.sbuf = sbuf
    core.scratch = scratch
    core.psum = psum
    core.banks = banks
    core.meet = meet
    core.ident = ident
    core.identb = identb
    core.center = center
    core.ones = ones
    core.xT = xT
    core.modT = modT
    core.gate = gate
    core.sq_ring = sq_ring
    core.inverse_root = inverse_root
    core.layer_norm = layer_norm

    with ExitStack() as scope:
        xtok = sbuf(scope, "xtok", [P, NT, P])
        theta = sbuf(scope, "theta", [P, 4, P])
        thetaT = sbuf(scope, "thetaT", [P, 4, P])
        cT = sbuf(scope, "cT", [P, 2, B])
        silu = sbuf(scope, "silu", [P, 3, 2, B])
        wmod = sbuf(scope, "wmod", [P, 2, 6 * P])
        brow = sbuf(scope, "brow", [1, B, P])
        upper = sbuf(scope, "upper", [P, 2, P])
        lower = sbuf(scope, "lower", [P, P])
        hT = sbuf(scope, "hT", [P, B, S])
        xc = sbuf(scope, "xc_ttt", [P, B, S])
        kT, qT = sbuf(scope, "kT_ttt", [P, B, S]), sbuf(scope, "qT_ttt", [P, B, S])
        ktok = sbuf(scope, "ktok", [P, NT, P])
        nat = sbuf(scope, "n_at", [P, NT, P])
        Y = sbuf(scope, "t_inv", [P, NT, P])
        PN = [sbuf(scope, f"pn{i}", [P, TPB, P]) for i in range(2)]
        PT_ = [sbuf(scope, f"pt{i}", [P, TPB, P]) for i in range(2)]
        WT = sbuf(scope, "WT", [P, B, P])
        R = sbuf(scope, "R", [P, B, P])
        U = sbuf(scope, "U", [P, B, P])

        for t in range(NT):
            first.start(SP, xtok[:, t, :], io["L0_attn_in_seq"].rearrange("b (c p) d -> p (b c) d", p=P)[:, t, :])
        for l, n in enumerate(("L0", "L1")):
            first.start(SP, wmod[:, l, :], io[n + "_wmod"])
            first.start(SP, cT[:, l, :], io[n + "_c"].rearrange("b d -> d b"))
        for j, n in enumerate(("theta_K", "theta_V", "theta_Q", "W0")):
            first.start(SP, theta[:, j, :], io["L0_attn_" + n])
        first.start(SP, upper[:, :, :], io["c_upper"])
        first.start(SP, lower[:, :], io["c_lower"])
        for b in range(B):
            first.start(SP, brow[:, b, :], io["L0_attn_b0"].rearrange("(a d) -> a d", a=1))
        loaded = first.mark()

        A.wait(loaded)
        m = A.did(A.e.activation(silu[:, 0, :, :], cT[:, :, :], ACT.Exp, scale=-1.0))
        V.wait(m, loaded)
        m = V.did(V.e.tensor_scalar(silu[:, 1, :, :], silu[:, 0, :, :], 1.0, None, ALU.add))
        V.wait(m)
        m = V.did(V.e.reciprocal(silu[:, 2, :, :], silu[:, 1, :, :]))
        V.wait(m)
        m = V.did(V.e.tensor_tensor(silu[:, 0, :, :], silu[:, 2, :, :], cT[:, :, :], ALU.mult))
        i, ps = banks.take(PE)
        PE.wait(loaded, m, o1)
        for l in range(2):
            for k in range(6):
                last = PE.e.matmul(ps[:, (l * 6 + k) * B:(l * 6 + k + 1) * B], wmod[:, l, k * P:(k + 1) * P],
                                   silu[:, 0, l, :], start=True, stop=True)
        m = PE.did(last)
        V.wait(m)
        m = V.did(V.e.tensor_copy(modT[:, :, :, :].rearrange("p l k b -> p (l k b)"), ps[:, 0:12 * B]))
        banks.done(i, m)
        for l in range(2):
            for n, k in enumerate((2, 5)):
                g = gate[:, l, n, :]
                twice, raw = rstd_tmp[:, 0:B], modT[:, l, k, :]
                V.wait(m)
                m = V.did(V.e.tensor_scalar(twice, raw, 0.0, 2.0, ALU.is_ge, ALU.mult))
                V.wait(m)
                m = V.did(V.e.scalar_tensor_tensor(out=g, in0=twice, scalar=-1.0, in1=raw, op0=ALU.add, op1=ALU.mult))
                V.wait(m)
                m = V.did(V.e.tensor_scalar(g, g, 0.25, None, ALU.max))
                V.wait(m)
                m = V.did(V.e.scalar_tensor_tensor(out=g, in0=twice, scalar=-1.0, in1=g, op0=ALU.add, op1=ALU.mult))
        V.wait(m)
        for l in range(2):
            for k in (1, 4):
                m = V.did(V.e.tensor_scalar(modT[:, l, k, :], modT[:, l, k, :], 1.0, None, ALU.add))
        mod_mark = m

        x_marks = []
        for b in range(B):
            i, ps = banks.take(PE)
            for c in range(TPB):
                last = PE.e.transpose(ps[:, c * P:(c + 1) * P], xtok[:, b * TPB + c, :], ident[:, :])
            m = PE.did(last)
            A.wait(m)
            m = A.did(A.e.activation(xT[:, b, :], ps, ACT.Copy))
            banks.done(i, m)
            x_marks.append(m)
        i, ps = banks.take(PE)
        for j in range(4):
            last = PE.e.transpose(ps[:, j * P:(j + 1) * P], theta[:, j, :], ident[:, :])
        m = PE.did(last)
        V.wait(m)
        for j in (0, 2):
            V.did(V.e.tensor_copy(thetaT[:, j, :], ps[:, j * P:(j + 1) * P]))
        V.did(V.e.tensor_scalar(thetaT[:, 1, :], ps[:, P:2 * P], -1.0, None, ALU.mult))
        m = V.did(V.e.tensor_copy(WT[:, :, :], ps[:, 3 * P:4 * P].unsqueeze(1).to_broadcast([P, B, P])))
        banks.done(i, m)
        theta_mark = m

        h_marks = []
        V.wait(mod_mark)
        for b in range(B):
            h_marks.append(layer_norm(hT[:, b, :], xT[:, b, :], xc[:, b, :], modT[:, 0, 1, b:b + 1], modT[:, 0, 0, b:b + 1], b, x_marks[b]))

        kq_marks, ktok_marks = [], []
        PE.wait(theta_mark)
        for b in range(B):
            PE.wait(h_marks[b])
            for j, dst in ((0, kT), (2, qT)):
                i, ps = banks.take(PE)
                m = PE.did(PE.e.matmul(ps, thetaT[:, j, :], hT[:, b, :], start=True, stop=True))
                A.wait(m)
                m = A.did(A.e.activation(dst[:, b, :], ps, ACT.Copy))
                banks.done(i, m)
            kq_marks.append(m)
            i, ps = banks.take(PE)
            for c in range(TPB):
                last = PE.e.matmul(ps[:, c * P:(c + 1) * P], hT[:, b, c * P:(c + 1) * P], thetaT[:, 0, :], start=True, stop=True)
            m = PE.did(last)
            V.wait(m)
            m = V.did(V.e.tensor_copy(ktok[:, b * TPB:(b + 1) * TPB, :].rearrange("p c d -> p (c d)"), ps))
            banks.done(i, m)
            ktok_marks.append(m)

        y_marks = []
        maskn = lambda ap: ap.unsqueeze(1).to_broadcast([P, TPB, P])
        pn_free = pt_free = None
        for b in range(B):
            bs = slice(b * TPB, (b + 1) * TPB)
            PE.wait(kq_marks[b])
            i, ps = banks.take(PE)
            for c in range(TPB):
                cs = slice(c * P, (c + 1) * P)
                last = PE.e.matmul(ps[:, cs], kT[:, b, cs], kT[:, b, cs], start=True, stop=True)
            m = PE.did(last)
            g3 = ps.rearrange("p (c t) -> p c t", c=TPB)
            V.wait(m, pn_free)
            m1 = V.did(V.e.scalar_tensor_tensor(out=PN[0][:, :, :], in0=g3, scalar=1.0, in1=maskn(lower[:, :]), op0=ALU.add, op1=ALU.mult))
            m2 = V.did(V.e.scalar_tensor_tensor(out=PT_[0][:, :, :], in0=g3, scalar=1.0, in1=maskn(upper[:, 0, :]), op0=ALU.add, op1=ALU.mult))
            banks.done(i, m2)
            V.wait(m2)
            my = V.did(V.e.tensor_tensor(Y[:, bs, :], maskn(ident[:, :]), PT_[0][:, :, :], ALU.subtract))
            i, ps = banks.take(PE)
            for c in range(TPB):
                cs = slice(c * P, (c + 1) * P)
                last = PE.e.matmul(ps[:, cs], kT[:, b, cs], qT[:, b, cs], start=True, stop=True)
            m = PE.did(last)
            V.wait(m)
            m = V.did(V.e.scalar_tensor_tensor(out=nat[:, bs, :], in0=ps.rearrange("p (c t) -> p c t", c=TPB), scalar=1.0,
                                               in1=maskn(upper[:, 1, :]), op0=ALU.add, op1=ALU.mult))
            banks.done(i, m)
            for j in range(6):
                n0, t0, n1, t1 = PN[j % 2], PT_[j % 2], PN[(j + 1) % 2], PT_[(j + 1) % 2]
                PE.wait(m1, m2)
                i, ps = banks.take(PE)
                for c in range(TPB):
                    last = PE.e.matmul(ps[:, c * P:(c + 1) * P], t0[:, c, :], n0[:, c, :], start=True, stop=True)
                m = PE.did(last)
                A.wait(m, my)
                m1n = A.did(A.e.activation(n1[:, :, :].rearrange("p c t -> p (c t)"), ps, ACT.Copy))
                banks.done(i, m1n)
                if j < 5:
                    i, ps = banks.take(PE)
                    for c in range(TPB):
                        last = PE.e.matmul(ps[:, c * P:(c + 1) * P], n0[:, c, :], t0[:, c, :], start=True, stop=True)
                    m = PE.did(last)
                    V.wait(m)
                    m2 = V.did(V.e.tensor_copy(t1[:, :, :].rearrange("p c t -> p (c t)"), ps))
                    banks.done(i, m2)
                m1 = m1n
                i, ps = banks.take(PE)
                PE.wait(m1, my)
                for c in range(TPB):
                    last = PE.e.matmul(ps[:, c * P:(c + 1) * P], n1[:, c, :], Y[:, b * TPB + c, :], start=True, stop=True)
                m = PE.did(last)
                V.wait(m)
                my = V.did(V.e.tensor_tensor(Y[:, bs, :], Y[:, bs, :], ps.rearrange("p (c t) -> p c t", c=TPB), ALU.add))
                banks.done(i, my)
            pn_free = m
            y_marks.append(my)

        w_mark, b_mark, u_free = theta_mark, loaded, None
        PE.wait(*ktok_marks, *y_marks)
        for c in range(TPB):
            cs = slice(c * P, (c + 1) * P)
            PE.wait(w_mark, b_mark)
            i, ps = banks.take(PE)
            for b in range(B):
                o = ps[:, b * P:(b + 1) * P]
                PE.e.matmul(o, kT[:, b, cs], WT[:, b, :], start=True, stop=False)
                PE.e.matmul(o, ones[0:1, :], brow[:, b, :], start=False, stop=False)
                last = PE.e.matmul(o, hT[:, b, cs], thetaT[:, 1, :], start=False, stop=True)
            m = PE.did(last)
            A.wait(m, u_free)
            r_mark = A.did(A.e.activation(R[:, :, :].rearrange("p b d -> p (b d)"), ps, ACT.Copy))
            banks.done(i, r_mark)
            i, ps = banks.take(PE)
            PE.wait(r_mark)
            for b in range(B):
                last = PE.e.matmul(ps[:, b * P:(b + 1) * P], Y[:, b * TPB + c, :], R[:, b, :], start=True, stop=True)
            m = PE.did(last)
            A.wait(m)
            u_mark = A.did(A.e.activation(U[:, :, :].rearrange("p b d -> p (b d)"), ps, ACT.Copy))
            banks.done(i, u_mark)
            i, ps = banks.take(PE)
            PE.wait(u_mark)
            for b in range(B):
                o = ps[:, b * P:(b + 1) * P]
                PE.e.matmul(o, WT[:, b, :], qT[:, b, cs], start=True, stop=False)
                PE.e.matmul(o, brow[:, b, :], ones[0:1, :], start=False, stop=False)
                last = PE.e.matmul(o, U[:, b, :], nat[:, b * TPB + c, :], start=False, stop=True)
            m = PE.did(last)
            V.wait(m)
            for b in range(B):
                x_mark = V.did(V.e.scalar_tensor_tensor(out=xT[:, b, cs], in0=ps[:, b * P:(b + 1) * P], scalar=gate[:, 0, 0, b:b + 1],
                                                        in1=xT[:, b, cs], op0=ALU.mult, op1=ALU.add))
            banks.done(i, x_mark)
            if c == TPB - 1:
                break
            i, ps = banks.take(PE)
            for b in range(B):
                last = PE.e.matmul(ps[:, b * P:(b + 1) * P], ktok[:, b * TPB + c, :], U[:, b, :], start=True, stop=True)
            m = PE.did(last)
            V.wait(m)
            w_mark = V.did(V.e.scalar_tensor_tensor(out=WT[:, :, :].rearrange("p b d -> p (b d)"), in0=ps, scalar=-ETA,
                                                    in1=WT[:, :, :].rearrange("p b d -> p (b d)"), op0=ALU.mult, op1=ALU.add))
            banks.done(i, w_mark)
            i, ps = banks.take(PE)
            for b in range(B):
                last = PE.e.matmul(ps[0:1, b * P:(b + 1) * P], ones[:, 0:1], U[:, b, :], start=True, stop=True)
            u_free = PE.did(last)
            V.wait(u_free)
            b_mark = V.did(V.e.scalar_tensor_tensor(out=brow[:, :, :].rearrange("p b d -> p (b d)"), in0=ps[0:1, :], scalar=-ETA,
                                                    in1=brow[:, :, :].rearrange("p b d -> p (b d)"), op0=ALU.mult, op1=ALU.add))
            banks.done(i, b_mark)
    meet()
    if stop > 0:
        transformer(core)
        meet()
    if stop > 1:
        relative_attention(core)
        meet()
    if stop > 2:
        experts(core)
        meet()

    with ExitStack() as scope:
        ytok = sbuf(scope, "ytok", [P, NT, P])
        stored = Loads(nc, "stored")
        out = io["out"].rearrange("b (c p) d -> p (b c) d", p=P)
        for b in range(B):
            i, ps = banks.take(PE)
            for c in range(TPB):
                last = PE.e.transpose(ps[:, c * P:(c + 1) * P], xT[:, b, c * P:(c + 1) * P], ident[:, :])
            m = PE.did(last)
            A.wait(m)
            m = A.did(A.e.activation(ytok[:, b * TPB:(b + 1) * TPB, :].rearrange("p c d -> p (c d)"), ps, ACT.Copy))
            banks.done(i, m)
            SP.wait(m)
            stored.start(SP, out[:, b * TPB:(b + 1) * TPB, :], ytok[:, b * TPB:(b + 1) * TPB, :])
        SP.wait(stored.mark())


def transformer(core):
    io, PE, V, A, G, SP, banks = core.io, core.PE, core.V, core.A, core.G, core.SP, core.banks
    ident, ones, xT, modT, gate = core.ident, core.ones, core.xT, core.modT, core.gate
    with ExitStack() as scope:
        def sb(name, shape, dt=F32):
            return core.sbuf(scope, name, shape, dt)

        z = sb("z", [P, B, S])
        xs = sb("xs", [P, B, WIN + S])
        wqkv = [sb(f"wqkv{i}", [P, 3 * INNER]) for i in range(2)]
        wo = [sb(f"wo{i}", [P, PAIRS, P]) for i in range(2)]
        w1 = [sb(f"w1_{i}", [P, 2 * DI]) for i in range(2)]
        w2 = [sb(f"w2_{i}", [P, 3, P]) for i in range(2)]
        cols = sb("cols", [P, 3, DEPTH])
        b1c = sb("b1c", [P, 2, 3, DEPTH])
        base = sb("rot_base", [P, 4, TPB, DH])
        rot = [sb(f"rot{i}", [P, 4, TPB, DH]) for i in range(2)]
        rows = sb("scale_rows", [1, 2, DEPTH, DH])
        scales = sb("scales", [P, 2, DEPTH, DH])
        mask = sb("mask", [P, 2, KB])
        maskb = sb("maskb", [P, 3, 2, KB], BF16)
        ss = Ring([sb(f"ss{i}", [P, 3, 2 * HEADS]) for i in range(2)])
        swap = sb("swap", [P, 2 * INNER])
        xc = swap[:, :].rearrange("p (b t) -> p b t", b=B)
        swap_ring = Ring([swap])
        a_ring = Ring([sb(f"qk{i}", [P, 2 * INNER]) for i in range(2)])
        q_ring = Ring([sb(f"qT{i}", [P, PAIRS, 2, P]) for i in range(2)])
        k_ring = Ring([sb(f"kT{i}", [P, PAIRS, WIN + P]) for i in range(3)])
        v_ring = Ring([sb(f"v{i}", [KB, 2, INNER]) for i in range(4)])
        p_ring = Ring([sb(f"p{i}", [P, PAIRS, 2, KB]) for i in range(2)])
        stat_ring = Ring([sb(f"stat{i}", [P, 3, HEADS]) for i in range(2)])
        pt_ring = Ring([sb(f"pT{i}", [KB, 2, 2, P]) for i in range(2)])
        o_ring = Ring([sb(f"oT{i}", [P, PAIRS, P]) for i in range(2)])

        once = Loads(core.nc, "ffn_once")
        once.start(SP, base[:, :, :, :], io["c_rot"])
        once.start(SP, mask[:, :, :], io["c_mask"])
        for j, n in enumerate(("ln_g", "ln_b", "b2")):
            once.start(SP, cols[:, j, :], io["L0_ffn_" + n].rearrange("l d -> d l"))
        for half in range(2):
            for j, (lo, n) in enumerate(CHUNKS):
                once.start(SP, b1c[0:n, half, j, :], io["L0_ffn_b1"][:, half * DI + lo:half * DI + lo + n].rearrange("l d -> d l"))
        for j, n in enumerate(("q_scale", "k_scale")):
            once.start(SP, rows[:, j, :, :], io["L0_ffn_" + n].rearrange("(a l) d -> a l d", a=1))
        weights = [Loads(core.nc, f"ffn_weights{i}") for i in range(2)]

        def load_layer(l, *free):
            SP.wait(*free)
            w = weights[l % 2]
            w.start(SP, wqkv[l % 2][:, :], io["L0_ffn_Wqkv"][l])
            w.start(SP, wo[l % 2][:, :, :], io["L0_ffn_Wo"][l].rearrange("(h p) d -> p h d", p=P))
            w.start(SP, w1[l % 2][:, :], io["L0_ffn_W1"][l])
            for j, (lo, n) in enumerate(CHUNKS):
                m = w.start(SP, w2[l % 2][0:n, j, :], io["L0_ffn_W2"][l, lo:lo + n, :])
            return m

        layer_loaded = {0: load_layer(0)}
        zero = G.did(G.e.memset(xs[:, :, :], 0.0))
        for q in q_ring.buffers:
            zero = G.did(G.e.memset(q[:, :, :, :], 0.0))
        A.wait(zero)
        V.wait(once.mark())
        V.did(V.e.tensor_copy(maskb[:, 0, 0, :], mask[:, 1, :]))
        V.did(V.e.tensor_copy(maskb[:, 0, 1, :], mask[:, 0, :]))
        V.did(V.e.tensor_copy(maskb[:, 1, :, :], mask[:, 0, :].unsqueeze(1).to_broadcast([P, 2, KB])))
        mask_mark = V.did(V.e.tensor_copy(core.identb[:, :], ident[:, :]))

        PE.wait(once.mark())
        for j in range(2):
            i, ps = banks.take(PE)
            m = PE.did(PE.e.matmul(ps[:, 0:DEPTH * DH], ones[0:1, :], rows[:, j, :, :].rearrange("a l d -> a (l d)"), start=True, stop=True))
            A.wait(m)
            scales_mark = A.did(A.e.activation(scales[:, j, :, :].rearrange("p l d -> p (l d)"), ps[:, 0:DEPTH * DH], ACT.Copy))
            banks.done(i, scales_mark)

        def rotary_tables(l, *free):
            G.wait(scales_mark, once.mark(), *free)
            for j in range(2):
                plain = scales[:, j, l, :].unsqueeze(1).to_broadcast([P, TPB, DH])
                swapped = scales[:, j, l, :].rearrange("p (a e) -> p a e", a=2)[:, ::-1, :]
                G.did(G.e.tensor_tensor(rot[l % 2][:, 2 * j, :, :], base[:, 2 * j, :, :], plain, ALU.mult))
                for c in range(TPB):
                    m = G.did(G.e.tensor_tensor(rot[l % 2][:, 2 * j + 1, c, :].rearrange("p (a e) -> p a e", a=2),
                                                base[:, 2 * j + 1, c, :].rearrange("p (a e) -> p a e", a=2), swapped, ALU.mult))
            return m

        def shift(b, *marks):
            A.wait(zero, *marks)
            V.wait(zero, *marks)
            h = P // 2
            m1 = A.did(A.e.activation(xs[0:h, b, WIN:WIN + S], z[0:h, b, :], ACT.Copy))
            m2 = V.did(V.e.tensor_copy(xs[h:P, b, WIN + 1:WIN + S], z[h:P, b, 0:S - 1]))
            return m1, m2

        def project(l, t, st):
            b, c = divmod(t, TPB)
            w, tab = wqkv[l % 2], rot[l % 2]
            PE.wait(layer_loaded[l], *st["xs"][b])
            here = xs[:, b, WIN + c * P:WIN + (c + 1) * P]
            held = []
            si, s2 = ss.take(V)
            for u in range(4):
                i, ps = banks.take(PE)
                m = PE.did(PE.e.matmul(ps, here, w[:, u * 512:(u + 1) * 512], start=True, stop=True))
                qi, sq = core.sq_ring.take(A)
                A.wait(m)
                m = A.did(A.e.activation(sq[:, :], ps, ACT.Square))
                V.wait(m)
                m = V.did(V.e.tensor_reduce(s2[:, 0, u * 8:(u + 1) * 8], sq[:, :].rearrange("p (h e) -> p h e", e=DH), AX, ALU.add))
                core.sq_ring.done(qi, m)
                held.append((i, ps))
                if u % 2:
                    yield
            V.wait(m)
            m = V.did(V.e.tensor_scalar(s2[:, 0, :], s2[:, 0, :], 1e-24, None, ALU.max))
            root = core.inverse_root(s2[:, 1, :], s2[:, 0, :], s2[:, 2, :], m, V)
            vi, v = v_ring.take(A)

            def windows(u):
                for half in range(2):
                    i, ps = banks.take(PE)
                    lo = c * P + u * QB
                    mp = PE.did(PE.e.matmul(ps[0:KB, :], xs[:, b, lo:lo + KB], w[:, 2 * INNER + half * 512:2 * INNER + (half + 1) * 512],
                                            start=True, stop=True))
                    A.wait(mp)
                    m = A.did(A.e.activation(v[:, u, half * 512:(half + 1) * 512], ps[0:KB, :], ACT.Copy))
                    banks.done(i, m)
                return mp, m

            ai, a = a_ring.take(V)
            bi, s = swap_ring.take(V)
            V.wait(root, st["tables"])
            for u in range(4):
                i, ps = held[u]
                m = V.did(V.e.tensor_tensor(a[:, u * 512:(u + 1) * 512].rearrange("p (h e) -> p h e", e=DH), ps.rearrange("p (h e) -> p h e", e=DH),
                                            s2[:, 1, u * 8:(u + 1) * 8].unsqueeze(2).to_broadcast([P, 8, DH]), ALU.mult))
                banks.done(i, m)
            V.wait(m)
            yield
            for j in range(2):
                part = slice(j * INNER, (j + 1) * INNER)
                a3, s3 = (x[:, part].rearrange("p (h e) -> p h e", e=DH) for x in (a, s))
                for half in range(2):
                    to, of = half * 32, (1 - half) * 32
                    V.did(V.e.tensor_tensor(s3[:, :, to:to + 32], a3[:, :, of:of + 32],
                                            tab[:, 2 * j + 1, c, to:to + 32].unsqueeze(1).to_broadcast([P, HEADS, 32]), ALU.mult))
                V.wait(V.last())
                m = V.did(V.e.tensor_tensor(a3, a3, tab[:, 2 * j, c, :].unsqueeze(1).to_broadcast([P, HEADS, DH]), ALU.mult))
                G.wait(m)
                m = G.did(G.e.tensor_tensor(a[:, part], a[:, part], s[:, part], ALU.add))
            ss.done(si, m)
            swap_ring.done(bi, m)
            st["rot"][t], st["rot_mark"][t] = (ai, a), m
            yield
            windows(0)
            yield
            mp, m = windows(1)
            st["v"][t], st["v_mark"][t], st["xs_read"] = (vi, v), m, mp

        def turn(l, t, st):
            c = t % TPB
            ai, a = st["rot"][t]
            qi, q = q_ring.take(A)
            ki, k = k_ring.take(A, G)
            if c == 0:
                km = G.did(G.e.memset(k[:, :, 0:WIN], 0.0))
            else:
                before = st["k"][t - 1][1]
                G.wait(st["k_mark"][t - 1])
                km = G.did(G.e.tensor_copy(k[:, :, 0:WIN], before[:, :, P:P + WIN]))
            PE.wait(st["rot_mark"][t])
            for g in range(4):
                i, ps = banks.take(PE)
                for e in range(4):
                    at = (g * 4 + e) * P
                    last = PE.e.transpose(ps[:, e * P:(e + 1) * P], a[:, at:at + P], ident[:, :])
                m = PE.did(last)
                A.wait(m)
                n = g % 2 * 4
                if g < 2:
                    for f in range(2):
                        fs = slice(f * DH, (f + 1) * DH)
                        ma = A.did(A.e.activation(q[fs, n:n + 4, :, fs], ps[fs, :].rearrange("p (h u t) -> p h u t", h=4, u=2), ACT.Copy))
                else:
                    ma = A.did(A.e.activation(k[:, n:n + 4, WIN:WIN + P], ps.rearrange("p (h t) -> p h t", h=4), ACT.Copy))
                banks.done(i, ma)
                yield
            a_ring.done(ai, m)
            st["q"][t], st["k"][t], st["k_mark"][t], st["kwin_mark"][t] = (qi, q), (ki, k), ma, km

        def attend(l, t, st):
            c = t % TPB
            (qi, q), (ki, k) = st["q"][t], st["k"][t]
            pi, p = p_ring.take(A, G)
            xi, stat = stat_ring.take(V, A)
            PE.wait(st["k_mark"][t], st["kwin_mark"][t], mask_mark)
            mk = maskb[:, 0 if c == 0 else 1, :, :]
            for g in range(PAIRS // 2):
                i, ps = banks.take(PE)
                PE.e.matmul(ps[:, 0:4 * KB].rearrange("p (h n) -> p h n", h=2), core.identb[:, :],
                            mk.rearrange("p u n -> p (u n)").unsqueeze(1).to_broadcast([P, 2, 2 * KB]), start=True, stop=False)
                for j in range(2):
                    for u in range(2):
                        at = (2 * j + u) * KB
                        last = PE.e.matmul(ps[:, at:at + KB], q[:, 2 * g + j, u, :], k[:, 2 * g + j, u * QB:u * QB + KB],
                                           start=False, stop=(j == 1 and u == 1))
                m = PE.did(last)
                four = slice(4 * g, 4 * g + 4)
                V.wait(m)
                m = V.did(V.e.tensor_reduce(stat[:, 0, four], ps[:, 0:4 * KB].rearrange("p (n k) -> p n k", n=4), AX, ALU.max, negate=True))
                A.wait(m)
                for n in range(4):
                    h = 4 * g + n
                    m = A.did(A.e.activation(p[:, 2 * g + n // 2, n % 2, :], ps[:, n * KB:(n + 1) * KB], ACT.Exp, bias=stat[:, 0, h:h + 1],
                                             accum_out=stat[:, 1, h:h + 1]))
                banks.done(i, m)
                V.wait(m)
                m = V.did(V.e.reciprocal(stat[:, 2, four], stat[:, 1, four]))
                G.wait(m)
                p4 = p[:, 2 * g:2 * g + 2, :, :].rearrange("p h u k -> p (h u) k")
                m = G.did(G.e.tensor_tensor(p4, p4, stat[:, 2, four].unsqueeze(2).to_broadcast([P, 4, KB]), ALU.mult))
                yield
            mq = PE.last()
            q_ring.done(qi, mq)
            st["k_users"][t] = mq
            stat_ring.done(xi, m)
            st["p"][t], st["p_mark"][t] = (pi, p), m

        def combine(l, t, st):
            b, c = divmod(t, TPB)
            (pi, p), (vi, v) = st["p"][t], st["v"][t]
            oi, o = o_ring.take(A)
            PE.wait(st["p_mark"][t], st["v_mark"][t])
            ready = []

            def weighted(g):
                ti, pt, mt = ready[g]
                PE.wait(mt)
                if g % 2 == 0:
                    st["bank"] = banks.take(PE)
                bi, po = st["bank"]
                for j in range(2):
                    for f in range(2):
                        h, fs = 2 * (2 * g + j) + f, slice(f * DH, (f + 1) * DH)
                        for u in range(2):
                            at = (g % 2 * 2 + j) * P + u * QB
                            last = PE.e.matmul(po[fs, at:at + QB], v[:, u, h * DH:(h + 1) * DH], pt[:, j, u, fs], start=True, stop=True)
                m = PE.did(last)
                pt_ring.done(ti, m)
                if g % 2:
                    A.wait(m)
                    m = A.did(A.e.activation(o[:, 2 * g - 2:2 * g + 2, :], po.rearrange("p (h t) -> p h t", h=4), ACT.Copy))
                    banks.done(bi, m)
                return m

            for g in range(PAIRS // 2):
                i, ps = banks.take(PE)
                for j in range(2):
                    for u in range(2):
                        last = PE.e.transpose(ps[0:KB, (2 * j + u) * P:(2 * j + u + 1) * P], p[:, 2 * g + j, u, :], ident[:, :])
                mp = PE.did(last)
                ti, pt = pt_ring.take(A)
                A.wait(mp)
                m = A.did(A.e.activation(pt[:, :, :, :].rearrange("k h u q -> k (h u q)"), ps[0:KB, :], ACT.Copy))
                banks.done(i, m)
                ready.append((ti, pt, m))
                if g:
                    weighted(g - 1)
                yield
            ma = weighted(g)
            p_ring.done(pi, mp)
            v_ring.done(vi, PE.last())
            yield
            i, ps = banks.take(PE)
            PE.wait(ma)
            for h in range(PAIRS):
                last = PE.e.matmul(ps[:, 0:P], wo[l % 2][:, h, :], o[:, h, :], start=(h == 0), stop=(h == PAIRS - 1))
            m = PE.did(last)
            o_ring.done(oi, m)
            zt = z[:, b, c * P:(c + 1) * P]
            V.wait(m)
            m = V.did(V.e.tensor_tensor(zt, zt, ps[:, 0:P], ALU.add))
            banks.done(i, m)
            st["z"][b] = m
            yield

        z_marks, xs_marks = [None] * B, [None] * B
        for b in range(B):
            z_marks[b] = core.layer_norm(z[:, b, :], xT[:, b, :], xc[:, b, :], modT[:, 0, 4, b:b + 1], modT[:, 0, 3, b:b + 1], b)
        for b in range(B):
            xs_marks[b] = shift(b, z_marks[b])

        for l in range(DEPTH):
            if l + 1 < DEPTH:
                layer_loaded[l + 1] = load_layer(l + 1, PE.last())
            st = {n: {} for n in ("v", "v_mark", "rot", "rot_mark", "q", "k", "k_mark", "kwin_mark", "k_users", "p", "p_mark", "z")}
            st["xs"], st["tables"] = xs_marks, rotary_tables(l, V.last())
            for step in range(NT + 3):
                running = [stage(l, step - lag, st) for stage, lag in ((combine, 3), (attend, 2), (turn, 1), (project, 0))
                           if 0 <= step - lag < NT]
                while running:
                    running = [r for r in running if next(r, False) is None]
                t = step - 2
                if 0 <= t < NT:
                    k_ring.done(st["k"][t][0], st["k_users"][t], st["kwin_mark"].get(t + 1))

            PE.wait(layer_loaded[l])
            for b in range(B):
                xs_marks[b] = shift(b, st["z"][b], st["xs_read"])
            A.wait(G.last())
            n_marks = [core.layer_norm(xc[:, b, :], xs[:, b, WIN:WIN + S], xc[:, b, :], cols[:, 0, l:l + 1], cols[:, 1, l:l + 1], b, *xs_marks[b])
                       for b in range(B)]
            w = w1[l % 2]
            for b in range(B):
                ai, act = a_ring.take(A, V)
                act = act[:, 0:3 * S].rearrange("p (j t) -> p j t", j=3)
                PE.wait(n_marks[b])
                for j, (lo, n) in enumerate(CHUNKS):
                    i, ps = banks.take(PE)
                    m = PE.did(PE.e.matmul(ps[0:n, :], w[:, DI + lo:DI + lo + n], xc[:, b, :], start=True, stop=True))
                    A.wait(m)
                    ma = A.did(A.e.activation(act[0:n, j, :], ps[0:n, :], ACT.Gelu, bias=b1c[0:n, 1, j, l:l + 1]))
                    banks.done(i, ma)
                    i, ps = banks.take(PE)
                    m = PE.did(PE.e.matmul(ps[0:n, :], w[:, lo:lo + n], xc[:, b, :], start=True, stop=True))
                    V.wait(m, ma)
                    mv = V.did(V.e.scalar_tensor_tensor(out=act[0:n, j, :], in0=ps[0:n, :], scalar=b1c[0:n, 0, j, l:l + 1],
                                                        in1=act[0:n, j, :], op0=ALU.add, op1=ALU.mult))
                    banks.done(i, mv)
                i, ps = banks.take(PE)
                PE.wait(mv)
                for j, (lo, n) in enumerate(CHUNKS):
                    last = PE.e.matmul(ps, w2[l % 2][0:n, j, :], act[0:n, j, :], start=(j == 0), stop=(j == 2))
                m = PE.did(last)
                a_ring.done(ai, m)
                V.wait(m)
                m = V.did(V.e.scalar_tensor_tensor(out=z[:, b, :], in0=ps, scalar=cols[:, 2, l:l + 1], in1=z[:, b, :], op0=ALU.add, op1=ALU.add))
                banks.done(i, m)
                if l + 1 < DEPTH:
                    xs_marks[b] = shift(b, m)
                else:
                    V.wait(m)
                    V.did(V.e.scalar_tensor_tensor(out=xT[:, b, :], in0=z[:, b, :], scalar=gate[:, 0, 1, b:b + 1], in1=xT[:, b, :],
                                                   op0=ALU.mult, op1=ALU.add))


def relative_attention(core):
    nc, io, PE, V, A, G, SP, banks = core.nc, core.io, core.PE, core.V, core.A, core.G, core.SP, core.banks
    ident, ones, xT, modT, gate = core.ident, core.ones, core.xT, core.modT, core.gate
    copy, isq = ACT.Copy, float(D2) ** -0.5
    mid = EXT // 2
    table_rows = 2 * M2 + 1
    q_dram, k_dram = (core.scratch(n, [3, P, B * S], BF16) for n in ("q_parts", "k_parts"))
    rk_dram = core.scratch("rel_k_parts", [3, D2, ROW], BF16)
    rv_dram = core.scratch("rel_v_ext", [ROW, D2])
    NQ = 4
    qr_dram = [core.scratch(f"by_position{i}", [H2, P, ROW]) for i in range(NQ)]
    o_dram = core.scratch("rel_values", [TPB, B * H2, P, D2])

    with ExitStack() as scope:
        def sb(name, shape, dt=F32):
            return core.sbuf(scope, name, shape, dt)

        vt = [sb(f"v_tok{i}", [P, NT, P]) for i in range(3)]
        woT = sb("woT2", [P, P])
        colb = sb("col_bias", [P, 4])
        rk = sb("rk", [KS, ROW], BF16)
        tv = sb("rel_v_window", [P, 3 * P, D2])
        once = Loads(nc, "rel_once")
        for j, n in enumerate(("bq", "bk", "bo")):
            once.start(SP, colb[:, j:j + 1], io["L1_attn_" + n].rearrange("(d a) -> d a", a=1))
        ext = Loads(nc, "rel_v_store")
        rel_v = io["L1_attn_rel_v"]
        ext.start(SP, rv_dram[mid - M2:mid + M2 + 1, :], rel_v)
        ext.start(SP, rv_dram[0:mid - M2, :], rel_v[0:1, :].to_broadcast([mid - M2, D2]))
        ext.start(SP, rv_dram[mid + M2 + 1:ROW, :], rel_v[table_rows - 1:table_rows, :].to_broadcast([ROW - mid - M2 - 1, D2]))
        SP.wait(ext.mark())
        once.start(SP, tv[:, :, :], bass.AP(rv_dram.tensor, 0, [[D2, P], [D2, 3 * P], [1, D2]]))

        with ExitStack() as early:
            def se(name, shape, dt=F32):
                return core.sbuf(early, name, shape, dt)

            wraw = se("w_raw", [P, 4, P])
            wT = se("wT2", [P, 3, P])
            hT, xc = se("hT2", [P, B, S]), se("xc2", [P, B, S])
            brow, evrow = se("bv_row", [1, P]), se("end_rows", [1, 2, D2])
            ends = se("ends", [P, 2, P])
            rkf = se("rkf", [D2, 2, ROW])
            part_ring = Ring([se(f"part{i}", [P, 2, S]) for i in range(2)])
            bf_ring = Ring([se(f"bf{i}", [P, 3, S], BF16) for i in range(2)])
            rkb = se("rkb", [D2, 3, ROW], BF16)
            for j, n in enumerate(("Wq", "Wk", "Wv", "Wo")):
                once.start(SP, wraw[:, j, :], io["L1_attn_" + n])
            once.start(SP, brow[:, :], io["L1_attn_bv"].rearrange("(a d) -> a d", a=1))
            once.start(SP, evrow[:, 0, :], rel_v[0:1, :])
            once.start(SP, evrow[:, 1, :], rel_v[table_rows - 1:table_rows, :])
            once.start(SP, rkf[:, 0, mid - M2:mid + M2 + 1], io["L1_attn_rel_k"].rearrange("t d -> d t"))
            loaded = once.mark()

            i, ps = banks.take(PE)
            PE.wait(loaded)
            for j in range(4):
                last = PE.e.transpose(ps[:, j * P:(j + 1) * P], wraw[:, j, :], ident[:, :])
            m = PE.did(last)
            V.wait(m)
            V.did(V.e.tensor_copy(wT[:, :, :].rearrange("p j d -> p (j d)"), ps[:, 0:3 * P]))
            w_mark = V.did(V.e.tensor_copy(woT[:, :], ps[:, 3 * P:4 * P]))
            banks.done(i, w_mark)
            i, ps = banks.take(PE)
            for j in range(2):
                last = PE.e.matmul(ps[:, j * D2:(j + 1) * D2], ones[0:1, :], evrow[:, j, :], start=True, stop=True)
            m = PE.did(last)
            V.wait(m)
            ends_mark = V.did(V.e.tensor_copy(ends[:, :, :].rearrange("p j (h d) -> p j h d", d=D2),
                                              ps[:, 0:2 * D2].rearrange("p (j d) -> p j d", j=2).unsqueeze(2).to_broadcast([P, 2, H2, D2])))
            banks.done(i, ends_mark)

            V.wait(loaded)
            lo, hi = mid - M2, mid + M2
            V.did(V.e.tensor_copy(rkf[:, 0, 0:lo], rkf[:, 0, lo:lo + 1].to_broadcast([D2, lo])))
            m = V.did(V.e.tensor_copy(rkf[:, 0, hi + 1:ROW], rkf[:, 0, hi:hi + 1].to_broadcast([D2, ROW - hi - 1])))
            V.wait(m)
            m = V.did(V.e.tensor_copy(rkb[:, 0, :], rkf[:, 0, :]))
            for j in range(2):
                V.wait(m)
                m = V.did(V.e.tensor_tensor(rkf[:, 1 - j, :], rkf[:, j, :], rkb[:, j, :], ALU.subtract))
                V.wait(m)
                m = V.did(V.e.tensor_copy(rkb[:, j + 1, :], rkf[:, 1 - j, :]))
            parts = [Loads(nc, f"parts_store{i}") for i in range(3)]
            SP.wait(m)
            parts[2].start(SP, rk_dram.rearrange("r d t -> d r t"), rkb[:, :, :])

            h_marks = [core.layer_norm(hT[:, b, :], xT[:, b, :], xc[:, b, :], modT[:, 1, 1, b:b + 1], modT[:, 1, 0, b:b + 1], b) for b in range(B)]
            PE.wait(w_mark)
            for b in range(B):
                PE.wait(h_marks[b])
                for j, dram in ((0, q_dram), (1, k_dram)):
                    i, ps = banks.take(PE)
                    m = PE.did(PE.e.matmul(ps, wT[:, j, :], hT[:, b, :], start=True, stop=True))
                    xi, part = part_ring.take(A, V)
                    bi, bf = bf_ring.take(V)
                    A.wait(m, loaded)
                    m = A.did(A.e.activation(part[:, 0, :], ps, ACT.Identity, bias=colb[:, j:j + 1]))
                    banks.done(i, m)
                    V.wait(m)
                    m = V.did(V.e.tensor_copy(bf[:, 0, :], part[:, 0, :]))
                    for r in range(2):
                        V.wait(m)
                        m = V.did(V.e.tensor_tensor(part[:, 1 - r, :], part[:, r, :], bf[:, r, :], ALU.subtract))
                        V.wait(m)
                        m = V.did(V.e.tensor_copy(bf[:, r + 1, :], part[:, 1 - r, :]))
                    part_ring.done(xi, m)
                    SP.wait(m)
                    bf_ring.done(bi, parts[bi].start(SP, dram[:, :, b * S:(b + 1) * S].rearrange("r p t -> p r t"), bf[:, :, :]))
                i, ps = banks.take(PE)
                for c in range(TPB):
                    o = ps[:, c * P:(c + 1) * P]
                    PE.e.matmul(o, hT[:, b, c * P:(c + 1) * P], wT[:, 2, :], start=True, stop=False)
                    last = PE.e.matmul(o, ones[0:1, :], brow[:, :], start=False, stop=True)
                m = PE.did(last)
                V.wait(m)
                bs = slice(b * TPB, (b + 1) * TPB)
                o3 = ps.rearrange("p (c d) -> p c d", c=TPB)
                m = V.did(V.e.tensor_copy(vt[0][:, bs, :], o3))
                V.wait(ends_mark)
                for j in range(2):
                    m = V.did(V.e.tensor_tensor(vt[1 + j][:, bs, :], o3, ends[:, j, :].unsqueeze(1).to_broadcast([P, TPB, P]), ALU.add))
                banks.done(i, m)
                v_mark = m
            SP.wait(*[x.mark() for x in parts])
            rk_loads = Loads(nc, "rk_loads")
            for r, (_, part) in enumerate(SPLITS):
                rk_mark = rk_loads.start(SP, rk[r * D2:(r + 1) * D2, :], rk_dram[part])
            core.meet()

        banks = Ring([core.psum[:, i, :] for i in range(7)])
        o_bank = core.psum[:, 7, :]
        HG = 2
        wtn = sb("w_near", [P, 3, B * H2, P])
        far_ring = Ring([sb(f"w_far{i}", [P, 2, P]) for i in range(2)])
        qp_ring = Ring([sb(f"qp{i}", [KS, H2, P], BF16) for i in range(2)])
        kp_ring = Ring([sb(f"kp{i}", [KS, H2 // 2, S], BF16) for i in range(2)])
        qr_ring = Ring([sb(f"qr{i}", [P, HG, ROW]) for i in range(2)])
        sh_ring = Ring([sb(f"shifted{i}", [P, HG, S]) for i in range(2)])
        sc_ring = Ring([sb(f"sc{i}", [P, HG, S]) for i in range(2)])
        mx_ring = Ring([sb(f"mx{i}", [P, 2, HG]) for i in range(4)])
        sums = sb("sums", [P, B, H2])
        rsum = sb("rsum", [P, B, H2])
        o_tok = sb("o_tok", [P, B, P])
        o_rel = sb("o_rel", [B * H2, 512])
        o_back = sb("o_back", [P, B * H2, D2])
        o_T = sb("o_T", [P, B, P])
        qp_loads = [Loads(nc, f"qp_loads{i}") for i in range(2)]
        kp_loads = [Loads(nc, f"kp_loads{i}") for i in range(2)]
        qr_stores = [Loads(nc, f"qr_stores{i}") for i in range(2)]
        sh_loads = [Loads(nc, f"shift_loads{i}") for i in range(2)]
        ov_store, ov_load = Loads(nc, "rel_values_store"), Loads(nc, "rel_values_load")
        PE.wait(rk_mark, v_mark)

        slot_read = {}
        groups = H2 // HG
        o_rel_free = o_back_free = o_tok_free = ot_free = near_free = None
        for it in range(TPB):
            near = [j for j in (it - 1, it, it + 1) if 0 <= j < TPB]
            far = [j for j in range(TPB) if j not in near]
            keys = slice(near[0] * P, (near[-1] + 1) * P)
            nk = len(near) * P
            V.wait(V.last())
            for n in range(2):
                si, sh = sh_ring.take(V)
                for j in far:
                    m = V.did(V.e.memset(sh[:, :, j * P:(j + 1) * P], 0.0))
                sh_ring.done(si, m)

            seq = [(b, g) for b in range(B) for g in range(groups)]
            state = {}

            def positions(n):
                b, g = seq[n]
                if g == 0:
                    qi, qp = qp_ring.take(SP)
                    at = b * S + it * P
                    for r, (part, _) in enumerate(SPLITS):
                        mark = qp_loads[qi].start(SP, qp[r * D2:(r + 1) * D2, :, :],
                                                  q_dram[part].rearrange("(h d) t -> d h t", d=D2)[:, :, at:at + P])
                    state["q", b] = (qi, qp, mark)
                slot = b % NQ
                qi, qp, mark = state["q", b]
                ri, qr = qr_ring.take(A, V)
                PE.wait(mark)
                for e in range(HG):
                    i, ps = banks.take(PE)
                    m = PE.did(PE.e.matmul(ps[:, 0:ROW], qp[:, g * HG + e, :], rk[:, :], start=True, stop=True))
                    A.wait(m)
                    m = A.did(A.e.activation(qr[:, e, :], ps[:, 0:ROW], copy))
                    banks.done(i, m)
                hs = slice(g * HG, (g + 1) * HG)
                SP.wait(m, *slot_read.get((it - 1, b), ()))
                stored = qr_stores[ri].start(SP, qr_dram[slot][hs].rearrange("h p t -> p h t"), qr[:, :, :])
                qr_ring.done(ri, stored)
                state["stored", n] = stored
                half = g // (groups // 2)
                if g % (groups // 2) == 0:
                    ki, kp = kp_ring.take(SP)
                    hs = slice(half * H2 // 2, (half + 1) * H2 // 2)
                    for r, (_, part) in enumerate(SPLITS):
                        mark = kp_loads[ki].start(SP, kp[r * D2:(r + 1) * D2, :, :],
                                                  k_dram[part].rearrange("(h d) t -> d h t", d=D2)[:, hs, b * S:(b + 1) * S])
                    state["k", b, half] = (ki, kp, mark)

            def fetch(n):
                b, g = seq[n]
                slot = b % NQ
                si, sh = sh_ring.take(SP)
                SP.wait(state["stored", n])
                start = g * HG * P * ROW + mid + (near[0] - it) * P
                src = bass.AP(qr_dram[slot].tensor, start, [[ROW - 1, P], [P * ROW, HG], [1, nk]])
                state["shifted", n] = (si, sh, sh_loads[si].start(SP, sh[:, :, keys], src))
                slot_read[it, b] = (state["shifted", n][2], *slot_read.get((it, b), ())[:1])

            def scores(n):
                b, g = seq[n]
                ki, kp, mark = state["k", b, g // (groups // 2)]
                qi, qp, _ = state["q", b]
                si, sh, sh_mark = state["shifted", n]
                ci, sc = sc_ring.take(V, A)
                xi, mx = mx_ring.take(V)
                PE.wait(mark)
                for e in range(HG):
                    h = g * HG + e
                    i, ps = banks.take(PE)
                    last = PE.e.matmul(ps, qp[:, h, :], kp[:, h % (H2 // 2), :], start=True, stop=not far)
                    for j in far:
                        edge = 0 if j < it else ROW - 1
                        last = PE.e.matmul(ps[:, j * P:(j + 1) * P], qp[:, h, :], rk[:, edge:edge + 1].to_broadcast([KS, P]),
                                           start=False, stop=(j == far[-1]))
                    mp = PE.did(last)
                    V.wait(mp, sh_mark)
                    m = V.did(V.e.tensor_tensor(sc[:, e, :], ps, sh[:, e, :], ALU.add))
                    banks.done(i, m)
                sh_ring.done(si, m)
                if g % (groups // 2) == groups // 2 - 1:
                    kp_ring.done(ki, mp)
                if g == groups - 1:
                    qp_ring.done(qi, mp)
                V.wait(m)
                m = V.did(V.e.tensor_reduce(mx[:, 0, :], sc[:, :, :], AX, ALU.max))
                V.wait(m)
                m = V.did(V.e.tensor_scalar(mx[:, 1, :], mx[:, 0, :], -isq, None, ALU.mult))
                A.wait(m, rsum_free)
                for e in range(HG):
                    h = g * HG + e
                    m = A.did(A.e.activation(sc[:, e, :], sc[:, e, :], ACT.Exp, bias=mx[:, 1, e:e + 1], scale=isq, accum_out=sums[:, b, h:h + 1]))
                mx_ring.done(xi, m)
                state["e", n] = (ci, sc, m)

            def values(n):
                b, g = seq[n]
                ci, sc, mark = state["e", n]
                if g == 0:
                    state["o", b] = o_bank[:, b * P:(b + 1) * P]
                PE.wait(mark)
                for e in range(HG):
                    h = g * HG + e
                    i, ps = banks.take(PE)
                    for j in range(TPB):
                        last = PE.e.transpose(ps[:, j * P:(j + 1) * P], sc[:, e, j * P:(j + 1) * P], ident[:, :])
                    mt = PE.did(last)
                    eng, cp = (A, lambda o, x: A.e.activation(o, x, copy)) if e % 2 else (V, lambda o, x: V.e.tensor_copy(o, x))
                    p3 = ps.rearrange("p (j t) -> p j t", j=TPB)
                    eng.wait(mt, near_free)
                    m = eng.did(cp(wtn[:, near[0] - it + 1:near[-1] - it + 2, b * H2 + h, :], p3[:, near[0]:near[-1] + 1, :]))
                    fi = None
                    if far:
                        fi, fw = far_ring.take(eng)
                        m = eng.did(cp(fw[:, 0:len(far), :], p3[:, far[0]:far[-1] + 1, :]))
                    banks.done(i, m)
                    PE.wait(m)
                    for j in range(TPB):
                        lhs = wtn[:, j - it + 1, b * H2 + h, :] if j in near else fw[:, j - far[0], :]
                        val = vt[0] if j in near else vt[1] if j < it else vt[2]
                        last = PE.e.matmul(state["o", b][:, h * D2:(h + 1) * D2], lhs, val[:, b * TPB + j, h * D2:(h + 1) * D2],
                                           start=(j == 0), stop=(j == TPB - 1))
                    m = PE.did(last)
                    if far:
                        far_ring.done(fi, m)
                sc_ring.done(ci, mt)
                state["pv"] = m

            rsum_free = state_free.get("sums") if it else None
            PE.wait(o_tok_free)
            for n in range(len(seq) + 3):
                for stage, lag in ((values, 3), (scores, 2), (fetch, 1), (positions, 0)):
                    if 0 <= n - lag < len(seq):
                        stage(n - lag)
            V.wait(state["pv"])
            m_tok = V.did(V.e.tensor_copy(o_tok[:, :, :].rearrange("p b d -> p (b d)"), o_bank))
            o_tok_free = m_tok
            per = 512 // D2
            for half in range(P // per):
                i, ps = banks.take(PE)
                for q in range(per):
                    il = half * per + q
                    for j in near:
                        v = 2 * M2 - 1 - il + (j - it) * P
                        last = PE.e.matmul(ps[0:B * H2, q * D2:(q + 1) * D2], wtn[:, j - it + 1, :, il], tv[:, v, :],
                                           start=(j == near[0]), stop=(j == near[-1]))
                m = PE.did(last)
                A.wait(m, o_rel_free)
                m = A.did(A.e.activation(o_rel[:, :], ps[0:B * H2, :], copy))
                banks.done(i, m)
                SP.wait(m)
                o_rel_free = ov_store.start(SP, o_dram[it][:, half * per:(half + 1) * per, :], o_rel[:, :].rearrange("h (q d) -> h q d", d=D2))
            near_free = PE.last()
            SP.wait(o_rel_free, o_back_free)
            back = ov_load.start(SP, o_back[:, :, :], o_dram[it].rearrange("h q d -> q h d"))
            V.wait(A.last(), m_tok)
            m = V.did(V.e.reciprocal(rsum[:, :, :], sums[:, :, :]))
            state_free = {"sums": m}
            V.wait(back, m)
            o4 = o_tok[:, :, :].rearrange("p b (h d) -> p (b h) d", d=D2)
            m = V.did(V.e.tensor_tensor(o4, o4, o_back[:, :, :], ALU.add))
            o_back_free = m
            V.wait(m)
            m = V.did(V.e.tensor_tensor(o4, o4, rsum[:, :, :].rearrange("p b h -> p (b h)").unsqueeze(2).to_broadcast([P, B * H2, D2]), ALU.mult))
            i, ps = banks.take(PE)
            PE.wait(m)
            for b in range(B):
                last = PE.e.transpose(ps[:, b * P:(b + 1) * P], o_tok[:, b, :], ident[:, :])
            m = PE.did(last)
            V.wait(m)
            m = V.did(V.e.tensor_copy(o_T[:, :, :].rearrange("p b t -> p (b t)"), ps))
            banks.done(i, m)
            i, ps = banks.take(PE)
            PE.wait(m)
            m = PE.did(PE.e.matmul(ps, woT[:, :], o_T[:, :, :].rearrange("p b t -> p (b t)"), start=True, stop=True))
            V.wait(m)
            m = V.did(V.e.tensor_scalar(o_T[:, :, :].rearrange("p b t -> p (b t)"), ps, colb[:, 2:3], None, ALU.add))
            banks.done(i, m)
            V.wait(m)
            for b in range(B):
                x = xT[:, b, it * P:(it + 1) * P]
                V.did(V.e.scalar_tensor_tensor(out=x, in0=o_T[:, b, :], scalar=gate[:, 1, 0, b:b + 1], in1=x, op0=ALU.mult, op1=ALU.add))
        for s in (*qr_stores, ov_store, *parts, ext):
            SP.wait(s.mark())


def experts(core):
    nc, io, PE, V, A, G, SP, banks = core.nc, core.io, core.PE, core.V, core.A, core.G, core.SP, core.banks
    ident, identb, xT, modT, gate, psum = core.ident, core.identb, core.xT, core.modT, core.gate, core.psum
    NJ = HD // P
    with ExitStack() as scope:
        def sb(name, shape, dt=F32):
            return core.sbuf(scope, name, shape, dt)

        hT, xc = sb("hT3", [P, B, S]), sb("xc3", [P, B, S])
        rw, rwT = sb("router", [NE, P]), sb("routerT", [P, NE])
        order = sb("order", [P, NE])
        logits, pick = sb("logits", [P, NT, NE]), sb("pick", [P, NT, NE])
        best = sb("best", [P, 2, NT])
        chosen = sb("chosen", [P, NT, NE], BF16)
        fc_ring = Ring([sb(f"fc{i}", [P, HD]) for i in range(3)])
        pr_ring = Ring([sb(f"pr{i}", [P, HD]) for i in range(3)])
        pT_ring = Ring([sb(f"prT{i}", [P, NJ, P]) for i in range(2)])
        xe_ring = Ring([sb(f"xe{i}", [P, S]) for i in range(3)])
        r_ring = Ring([sb(f"relu{i}", [P, S]) for i in range(3)])
        s_ring = Ring([sb(f"square{i}", [P, S]) for i in range(3)])
        loads = Loads(nc, "router_load")
        loads.start(SP, rw[:, :], io["L1_ffn_router_w"])
        loads.start(SP, order[:, :], io["c_first"])
        w_loads = [Loads(nc, f"expert_loads{i}") for i in range(3)]
        w_marks = {}

        def load(e, *free):
            fi, fc = fc_ring.take(SP)
            ri, pr = pr_ring.take(SP)
            w_loads[e % 3].start(SP, fc[:, :], io["L1_ffn_expert_fc"][e])
            w_marks[e] = (fi, fc, ri, pr, w_loads[e % 3].start(SP, pr[:, :], io["L1_ffn_expert_proj"][e]))

        for e in range(2):
            load(e)
        m = V.did(V.e.tensor_copy(identb[:, :], ident[:, :]))
        PE.wait(m, loads.mark())
        i, ps = banks.take(PE)
        m = PE.did(PE.e.transpose(ps[:, 0:NE], rw[:, :], ident[0:NE, 0:NE]))
        V.wait(m, loads.mark())
        m = V.did(V.e.tensor_copy(rwT[:, :], ps[:, 0:NE]))
        banks.done(i, m)
        PE.wait(m)
        h_marks = [core.layer_norm(hT[:, b, :], xT[:, b, :], xc[:, b, :], modT[:, 1, 4, b:b + 1], modT[:, 1, 3, b:b + 1], b) for b in range(B)]
        i, ps = banks.take(PE)
        PE.wait(*h_marks)
        for t in range(NT):
            b, c = divmod(t, TPB)
            last = PE.e.matmul(ps[:, t * NE:(t + 1) * NE], hT[:, b, c * P:(c + 1) * P], rwT[:, :], start=True, stop=True)
        m = PE.did(last)
        V.wait(m)
        m = V.did(V.e.tensor_copy(logits[:, :, :].rearrange("p t e -> p (t e)"), ps[:, 0:NT * NE]))
        banks.done(i, m)
        wide = lambda j: best[:, j, :].unsqueeze(2).to_broadcast([P, NT, NE])
        V.wait(m)
        m = V.did(V.e.tensor_reduce(best[:, 0, :], logits[:, :, :], AX, ALU.max))
        V.wait(m)
        m = V.did(V.e.tensor_tensor(pick[:, :, :], logits[:, :, :], wide(0), ALU.is_ge))
        V.wait(m)
        m = V.did(V.e.tensor_tensor(pick[:, :, :], pick[:, :, :], order[:, :].unsqueeze(1).to_broadcast([P, NT, NE]), ALU.mult))
        V.wait(m)
        m = V.did(V.e.tensor_reduce(best[:, 1, :], pick[:, :, :], AX, ALU.max))
        V.wait(m)
        m = V.did(V.e.tensor_tensor(chosen[:, :, :], pick[:, :, :], wide(1), ALU.is_equal))
        chosen_mark = m

        work = [(e, b) for e in range(NE) for b in range(B)]
        core.meet()
        small = Ring([psum[:, i, :] for i in range(4)])
        sums = [psum[:, 4 + b, :] for b in range(B)]
        masked, turned = {}, {}

        def prepare(n):
            e, b = work[n]
            if b == 0:
                if 1 <= e < NE - 1:
                    load(e + 1)
                fi, fc, ri, pr, mark = w_marks[e]
                i, ps = small.take(PE)
                PE.wait(mark)
                for j in range(NJ):
                    last = PE.e.transpose(ps[:, j * P:(j + 1) * P], pr[:, j * P:(j + 1) * P], ident[:, :])
                m = PE.did(last)
                pr_ring.done(ri, m)
                ti, pT = pT_ring.take(A)
                A.wait(m)
                m = A.did(A.e.activation(pT[:, :, :].rearrange("p j d -> p (j d)"), ps, ACT.Copy))
                small.done(i, m)
                turned[e] = (ti, pT, m)
            i, ps = small.take(PE)
            PE.wait(chosen_mark)
            for c in range(TPB):
                last = PE.e.matmul(ps[:, c * P:(c + 1) * P], chosen[:, b * TPB + c, e:e + 1].to_broadcast([P, P]), identb[:, :], start=True, stop=True)
            m = PE.did(last)
            xi, xe = xe_ring.take(V)
            V.wait(m)
            m = V.did(V.e.tensor_tensor(xe[:, :], hT[:, b, :], ps, ALU.mult))
            small.done(i, m)
            masked[n] = (xi, xe, m)

        hidden = {}

        def up(n, j):
            e, b = work[n]
            fi, fc, _, _, _ = w_marks[e]
            xi, xe, mark = masked[n]
            i, ps = small.take(PE)
            PE.wait(mark)
            m = PE.did(PE.e.matmul(ps, fc[:, j * P:(j + 1) * P], xe[:, :], start=True, stop=True))
            if j == NJ - 1:
                xe_ring.done(xi, m)
                if b == B - 1:
                    fc_ring.done(fi, m)
            ri, r = r_ring.take(V)
            V.wait(m)
            m = V.did(V.e.tensor_scalar(r[:, :], ps, 0.0, None, ALU.max))
            small.done(i, m)
            si, s = s_ring.take(A)
            A.wait(m)
            m = A.did(A.e.activation(s[:, :], r[:, :], ACT.Square))
            r_ring.done(ri, m)
            hidden[n, j] = (si, s, m)

        def down(n, j):
            e, b = work[n]
            ti, pT, mark = turned[e]
            si, s, m = hidden[n, j]
            PE.wait(mark, m)
            m = PE.did(PE.e.matmul(sums[b], pT[:, j, :], s[:, :], start=(e == 0 and j == 0), stop=(e == NE - 1 and j == NJ - 1)))
            s_ring.done(si, m)
            if b == B - 1 and j == NJ - 1:
                pT_ring.done(ti, m)
            return m

        steps = [(n, j) for n in range(len(work)) for j in range(NJ)]
        prepare(0)
        lag = 2
        for k in range(len(steps) + lag):
            if k < len(steps):
                n, j = steps[k]
                if j == 1 and n + 1 < len(work):
                    prepare(n + 1)
                up(n, j)
            if k >= lag:
                m = down(*steps[k - lag])
        V.wait(m)
        for b in range(B):
            V.did(V.e.scalar_tensor_tensor(out=xT[:, b, :], in0=sums[b], scalar=gate[:, 1, 1, b:b + 1], in1=xT[:, b, :], op0=ALU.mult, op1=ALU.add))
        core.meet()


def constants():
    f = np.float32
    half = np.arange(0, DH, 2, dtype=f)
    inv_freq = (f(1.0) / f(10000.0) ** (half / f(DH))).astype(f)
    pos = np.arange(S, dtype=f)
    freqs = np.concatenate([pos[:, None] * inv_freq[None, :]] * 2, -1)
    power = (pos - S // 2) / f(WIN // 2)
    scale = ((half + f(0.4 * DH)) / f(1.4 * DH))[None, :] ** power[:, None]
    scale = np.concatenate([scale, scale], -1).astype(np.float64)
    sign = np.where(np.arange(DH) < DH // 2, -1.0, 1.0)
    cos, sin = np.cos(freqs.astype(np.float64)), np.sin(freqs.astype(np.float64)) * sign
    rot = np.stack([8.0 * cos * scale, 8.0 * sin * scale, cos / scale, sin / scale])
    rot = rot.reshape(4, TPB, P, DH).transpose(2, 0, 1, 3)
    i, j = np.arange(QB)[:, None], np.arange(KB)[None, :] - WIN
    ok = (j <= i) & (j >= i - WIN)
    mask = np.stack([ok, ok & (j >= 0)], 1)
    mask = np.where(np.concatenate([mask, mask]), 0.0, MASKED)
    up = np.triu(np.ones((P, P)), 1) * ETA
    eye = np.eye(P)
    out = {
        "c_ident": eye, "c_center": eye - 1.0 / P, "c_lower": up.T,
        "c_upper": np.stack([up, -(up + eye * ETA)], 1), "c_rot": rot, "c_mask": mask,
        "c_first": np.broadcast_to(NE - np.arange(NE), (P, NE)),
    }
    return {n: np.ascontiguousarray(a, dtype=f) for n, a in out.items()}


def kernel(**inputs):
    import concourse.bacc as bacc
    from concourse.bass_utils import run_bass_kernel_spmd

    nc = bacc.Bacc("TRN2", target_bir_lowering=False, num_devices=1)
    arrays = {n: np.ascontiguousarray(a) for n, a in inputs.items()}
    arrays.update(constants())
    io = {n: nc.dram_tensor(n, a.shape, mybir.dt.from_np(a.dtype), kind="ExternalInput").ap() for n, a in arrays.items()}
    io["out"] = nc.dram_tensor("out", (B, S, P), F32, kind="ExternalOutput").ap()
    build(nc, io)
    result = run_bass_kernel_spmd(nc, [arrays], core_ids=[0])
    return result.results[0]["out"]
```

```python
from contextlib import ExitStack

import numpy as np

import concourse.bass as bass
from concourse import mybir

F32 = mybir.dt.float32
BF16 = mybir.dt.bfloat16
F32R = mybir.dt.float32r
I32 = mybir.dt.int32
ALU = mybir.AluOpType
ACT = mybir.ActivationFunctionType
AX = mybir.AxisListType.X

P = 128
B, S = 4, 512
NT = B * S // P
TPB = S // P
LN_EPS = 1e-5
ETA = 0.01 * 2.0 / P
DEPTH, HEADS, DH, WIN = 6, 16, 64, 32
INNER = HEADS * DH
PAIRS = HEADS // 2
QB = 64
KB = QB + WIN
DI = int(P * 4 * 2 / 3)
CHUNKS = [(0, 128), (128, 128), (256, DI - 256)]
MASKED = -1e30
H2 = 16
D2 = P // H2
M2 = 128
EXT = 2 * 2 * M2 - 1
ROW = 512
SPLITS = [(a, b) for b in range(3) for a in range(3)]
SLOTS = 8
KS = len(SPLITS) * D2
NE, HD = 8, 512


class Engine:

    def __init__(self, nc, engine, name):
        self.e, self.name, self.sem = engine, name, nc.alloc_semaphore(name + "_done")
        self.count, self.seen = 0, {}

    def wait(self, *marks):
        for sem, value, name in [m for m in marks if m is not None]:
            if self.seen.get(name, 0) < value:
                self.e.wait_ge(sem, value)
                self.seen[name] = value

    def did(self, instruction):
        self.count += 1
        instruction.then_inc(self.sem, 1)
        return (self.sem, self.count, self.name)

    def last(self):
        return (self.sem, self.count, self.name) if self.count else None


class Loads:

    def __init__(self, nc, name):
        self.name, self.sem, self.count = name, nc.alloc_semaphore(name), 0

    def start(self, engine, out, in_):
        self.count += 16
        engine.e.dma_start(out, in_).then_inc(self.sem, 16)
        return self.mark()

    def mark(self):
        return (self.sem, self.count, self.name)


class Ring:

    def __init__(self, buffers):
        self.buffers, self.users, self.idle = buffers, [()] * len(buffers), list(range(len(buffers)))

    def take(self, *writers):
        i = self.idle.pop(0)
        for w in writers:
            w.wait(*self.users[i])
        return i, self.buffers[i]

    def done(self, i, *marks):
        assert i not in self.idle
        self.users[i] = marks
        self.idle.append(i)


class Core:
    pass


def build(nc, io):
    with ExitStack() as whole:
        whole.enter_context(nc.allow_non_contiguous_dma(reason="small vectors loaded as columns"))
        build_body(nc, io, whole)


def build_body(nc, io, whole):
    PE, V = Engine(nc, nc.tensor, "pe"), Engine(nc, nc.vector, "dve")
    A, G = Engine(nc, nc.scalar, "act"), Engine(nc, nc.gpsimd, "pool")
    SP = Engine(nc, nc.sync, "sp")
    compute = (PE, V, A, G)

    def sbuf(stack, name, shape, dt=F32):
        return stack.enter_context(nc.sbuf_tensor(name, shape, dt))

    def scratch(name, shape, dt=F32):
        return nc.dram_tensor(name, shape, dt, kind="Internal").ap()

    psum = whole.enter_context(nc.psum_tensor("psum", [P, 8, 512], F32))
    banks = Ring([psum[:, i, :] for i in range(8)])

    def meet():
        marks = [x.last() for x in compute]
        for x in (*compute, SP):
            x.wait(*marks)

    ident = sbuf(whole, "ident", [P, P])
    identb = sbuf(whole, "identb", [P, P], BF16)
    center = sbuf(whole, "center", [P, P])
    center_r = sbuf(whole, "center_r", [P, P], F32R)
    ones = sbuf(whole, "ones", [P, P])
    xT = sbuf(whole, "xT", [P, B, S])
    modT = sbuf(whole, "modT", [P, 2, 6, B])
    gate = sbuf(whole, "gate", [P, 2, 2, B])
    rstd_tmp = sbuf(whole, "rstd_tmp", [P, 16])
    rstd = sbuf(whole, "rstd", [P, B, TPB])
    rstd_in = sbuf(whole, "rstd_in", [P, B, TPB])
    sq_ring = Ring([sbuf(whole, f"sq{i}", [P, 512]) for i in range(2)])

    first = Loads(nc, "first_loads")
    for dst, src in ((ident, "c_ident"), (center, "c_center")):
        first.start(SP, dst[:, :], io[src])
    o1 = V.did(V.e.memset(ones[:, :], 1.0))

    def inverse_root(y, x, t, x_mark, eng):
        V.wait(x_mark)
        m = V.did(V.e.tensor_scalar(t.bitcast(I32), x.bitcast(I32), 1, None, ALU.logical_shift_right))
        V.wait(m)
        m = V.did(V.e.tensor_scalar(y.bitcast(I32), t.bitcast(I32), -1.0, float(0x5F3759DF), ALU.mult, ALU.add))
        mult, add = ALU.mult, ALU.add
        for _ in range(3):
            eng.wait(m)
            m = eng.did(eng.e.tensor_tensor(t, y, y, mult))
            if eng is V:
                for out, in0, scalar, op, in1 in ((t, t, -0.5, mult, x), (y, t, 1.5, add, y)):
                    eng.wait(m)
                    m = eng.did(eng.e.scalar_tensor_tensor(out=out, in0=in0, scalar=scalar, in1=in1, op0=op, op1=mult))
            else:
                eng.wait(m)
                m = eng.did(eng.e.tensor_tensor(t, t, x, mult))
                eng.wait(m)
                m = eng.did(eng.e.tensor_scalar(t, t, -0.5, 1.5, mult, add))
                eng.wait(m)
                m = eng.did(eng.e.tensor_tensor(y, y, t, mult))
        return m

    rstd_users = [()] * B

    def layer_norm_steps(dst, src, xc, scale, shift, k, *src_marks):
        i, ps = banks.take(PE)
        PE.wait(*src_marks)
        if isinstance(src, tuple):
            PE.e.matmul(ps, center_r[:, :], src[1], start=True, stop=False)
            m = PE.did(PE.e.matmul(ps, center_r[:, :], src[0], start=False, stop=True))
        else:
            m = PE.did(PE.e.matmul(ps, center[:, :], src, start=True, stop=True))
        yield
        si, sq = sq_ring.take(A)
        A.wait(m)
        A.did(A.e.activation(xc, ps, ACT.Copy))
        m = A.did(A.e.activation(sq[:, :], ps, ACT.Square))
        banks.done(i, m)
        xc_mark = m
        yield
        i, ps = banks.take(PE)
        PE.wait(m)
        for c in range(TPB):
            last = PE.e.matmul(ps[:, c:c + 1], sq[:, c * P:(c + 1) * P], ones[:, 0:1], start=True, stop=True)
        m = PE.did(last)
        sq_ring.done(si, m)
        yield
        var, r = rstd_in[:, k, 0:TPB], rstd[:, k, 0:TPB]
        V.wait(m, *rstd_users[k])
        m = V.did(V.e.tensor_scalar(var, ps[:, 0:TPB], 1.0 / P, LN_EPS, ALU.mult, ALU.add))
        banks.done(i, m)
        m = inverse_root(r, var, rstd_tmp[:, k * TPB:(k + 1) * TPB], m, V)
        yield
        i, ps = banks.take(PE)
        PE.wait(m)
        for c in range(TPB):
            last = PE.e.matmul(ps[:, c * P:(c + 1) * P], r[:, c:c + 1].to_broadcast([P, P]), ident[:, :], start=True, stop=True)
        m = PE.did(last)
        rstd_users[k] = (m,)
        yield
        V.wait(m, xc_mark)
        m = V.did(V.e.tensor_tensor(xc, xc, ps, ALU.mult))
        banks.done(i, m)
        V.wait(m)
        return V.did(V.e.tensor_scalar(dst, xc, scale, shift, ALU.mult, ALU.add))

    def side_by_side(steps):
        results, running, turns = [None] * len(steps), dict(enumerate(steps)), 0
        while running:
            turns += 1
            for n in [n for n in running if n < turns]:
                try:
                    next(running[n])
                except StopIteration as end:
                    results[n] = end.value
                    del running[n]
        return results

    core = Core()
    core.nc = nc
    core.io = io
    core.PE = PE
    core.V = V
    core.A = A
    core.G = G
    core.SP = SP
    core.sbuf = sbuf
    core.scratch = scratch
    core.psum = psum
    core.banks = banks
    core.meet = meet
    core.ident = ident
    core.identb = identb
    core.center = center
    core.center_r = center_r
    core.ones = ones
    core.xT = xT
    core.modT = modT
    core.gate = gate
    core.sq_ring = sq_ring
    core.inverse_root = inverse_root
    core.layer_norm_steps = layer_norm_steps
    core.side_by_side = side_by_side

    with ExitStack() as scope:
        xtok = sbuf(scope, "xtok", [P, NT, P])
        theta = sbuf(scope, "theta", [P, 4, P])
        thetaT = sbuf(scope, "thetaT", [P, 4, P])
        cT = sbuf(scope, "cT", [P, 2, B])
        silu = sbuf(scope, "silu", [P, 3, 2, B])
        wmod = sbuf(scope, "wmod", [P, 2, 6 * P])
        brow = sbuf(scope, "brow", [1, B, P])
        upper = sbuf(scope, "upper", [P, 2, P])
        lower = sbuf(scope, "lower", [P, P])
        hT = sbuf(scope, "hT", [P, B, S])
        xc = sbuf(scope, "xc_ttt", [P, B, S])
        kT, qT = sbuf(scope, "kT_ttt", [P, B, S]), sbuf(scope, "qT_ttt", [P, B, S])
        ktok = sbuf(scope, "ktok", [P, NT, P])
        nat = sbuf(scope, "n_at", [P, NT, P])
        Y = sbuf(scope, "t_inv", [P, NT, P])
        PN = [sbuf(scope, f"pn{i}", [P, TPB, P]) for i in range(2)]
        PT_ = [sbuf(scope, f"pt{i}", [P, TPB, P]) for i in range(2)]
        WT = sbuf(scope, "WT", [P, B, P])
        R = sbuf(scope, "R", [P, B, P])
        U = sbuf(scope, "U", [P, B, P])

        x_loaded = first.start(SP, xtok[:, :, :], io["L0_attn_in_seq"].rearrange("b (c p) d -> p (b c) d", p=P))
        first = Loads(nc, "first_weights")
        for l, n in enumerate(("L0", "L1")):
            first.start(SP, wmod[:, l, :], io[n + "_wmod"])
            first.start(SP, cT[:, l, :], io[n + "_c"].rearrange("b d -> d b"))
        for j, n in enumerate(("theta_K", "theta_V", "theta_Q", "W0")):
            first.start(SP, theta[:, j, :], io["L0_attn_" + n])
        first.start(SP, upper[:, :, :], io["c_upper"])
        first.start(SP, lower[:, :], io["c_lower"])
        first.start(SP, brow[:, :, :], io["L0_attn_b0"].rearrange("(a b d) -> a b d", a=1, b=1).to_broadcast([1, B, P]))
        loaded = first.mark()

        x_marks = []
        PE.wait(x_loaded, o1)
        for b in range(B):
            i, ps = banks.take(PE)
            for c in range(TPB):
                last = PE.e.transpose(ps[:, c * P:(c + 1) * P], xtok[:, b * TPB + c, :], ident[:, :])
            m = PE.did(last)
            A.wait(m)
            m = A.did(A.e.activation(xT[:, b, :], ps, ACT.Copy))
            banks.done(i, m)
            x_marks.append(m)

        A.wait(loaded)
        m = A.did(A.e.activation(silu[:, 0, :, :], cT[:, :, :], ACT.Exp, scale=-1.0))
        V.wait(m, loaded)
        m = V.did(V.e.tensor_scalar(silu[:, 1, :, :], silu[:, 0, :, :], 1.0, None, ALU.add))
        V.wait(m)
        m = V.did(V.e.reciprocal(silu[:, 2, :, :], silu[:, 1, :, :]))
        V.wait(m)
        m = V.did(V.e.tensor_tensor(silu[:, 0, :, :], silu[:, 2, :, :], cT[:, :, :], ALU.mult))
        i, ps = banks.take(PE)
        PE.wait(loaded, m, o1)
        for l in range(2):
            for k in range(6):
                last = PE.e.matmul(ps[:, (l * 6 + k) * B:(l * 6 + k + 1) * B], wmod[:, l, k * P:(k + 1) * P],
                                   silu[:, 0, l, :], start=True, stop=True)
        m = PE.did(last)
        V.wait(m)
        m = V.did(V.e.tensor_copy(modT[:, :, :, :].rearrange("p l k b -> p (l k b)"), ps[:, 0:12 * B]))
        banks.done(i, m)
        for l in range(2):
            for n, k in enumerate((2, 5)):
                g = gate[:, l, n, :]
                twice, raw = rstd_tmp[:, 0:B], modT[:, l, k, :]
                V.wait(m)
                m = V.did(V.e.tensor_scalar(twice, raw, 0.0, 2.0, ALU.is_ge, ALU.mult))
                V.wait(m)
                m = V.did(V.e.scalar_tensor_tensor(out=g, in0=twice, scalar=-1.0, in1=raw, op0=ALU.add, op1=ALU.mult))
                V.wait(m)
                m = V.did(V.e.tensor_scalar(g, g, 0.25, None, ALU.max))
                V.wait(m)
                m = V.did(V.e.scalar_tensor_tensor(out=g, in0=twice, scalar=-1.0, in1=g, op0=ALU.add, op1=ALU.mult))
        V.wait(m)
        for l in range(2):
            for k in (1, 4):
                m = V.did(V.e.tensor_scalar(modT[:, l, k, :], modT[:, l, k, :], 1.0, None, ALU.add))
        mod_mark = m

        i, ps = banks.take(PE)
        for j in range(4):
            last = PE.e.transpose(ps[:, j * P:(j + 1) * P], theta[:, j, :], ident[:, :])
        m = PE.did(last)
        V.wait(m)
        for j in (0, 2):
            V.did(V.e.tensor_copy(thetaT[:, j, :], ps[:, j * P:(j + 1) * P]))
        V.did(V.e.tensor_scalar(thetaT[:, 1, :], ps[:, P:2 * P], -1.0, None, ALU.mult))
        m = V.did(V.e.tensor_copy(WT[:, :, :], ps[:, 3 * P:4 * P].unsqueeze(1).to_broadcast([P, B, P])))
        banks.done(i, m)
        theta_mark = m

        V.wait(mod_mark)
        h_marks = side_by_side([layer_norm_steps(hT[:, b, :], xT[:, b, :], xc[:, b, :], modT[:, 0, 1, b:b + 1], modT[:, 0, 0, b:b + 1],
                                                 b, x_marks[b]) for b in range(B)])

        kq_marks, ktok_marks = [], []
        PE.wait(theta_mark)
        for b in range(B):
            PE.wait(h_marks[b])
            for j, dst in ((0, kT), (2, qT)):
                i, ps = banks.take(PE)
                m = PE.did(PE.e.matmul(ps, thetaT[:, j, :], hT[:, b, :], start=True, stop=True))
                A.wait(m)
                m = A.did(A.e.activation(dst[:, b, :], ps, ACT.Copy))
                banks.done(i, m)
            kq_marks.append(m)
            i, ps = banks.take(PE)
            for c in range(TPB):
                last = PE.e.matmul(ps[:, c * P:(c + 1) * P], hT[:, b, c * P:(c + 1) * P], thetaT[:, 0, :], start=True, stop=True)
            m = PE.did(last)
            V.wait(m)
            m = V.did(V.e.tensor_copy(ktok[:, b * TPB:(b + 1) * TPB, :].rearrange("p c d -> p (c d)"), ps))
            banks.done(i, m)
            ktok_marks.append(m)

        y_marks = []
        maskn = lambda ap: ap.unsqueeze(1).to_broadcast([P, TPB, P])
        pn_free = None
        for b in range(B):
            bs = slice(b * TPB, (b + 1) * TPB)
            PE.wait(kq_marks[b])
            i, ps = banks.take(PE)
            for c in range(TPB):
                cs = slice(c * P, (c + 1) * P)
                last = PE.e.matmul(ps[:, cs], kT[:, b, cs], kT[:, b, cs], start=True, stop=True)
            m = PE.did(last)
            g3 = ps.rearrange("p (c t) -> p c t", c=TPB)
            V.wait(m, pn_free)
            m1 = V.did(V.e.scalar_tensor_tensor(out=PN[0][:, :, :], in0=g3, scalar=1.0, in1=maskn(lower[:, :]), op0=ALU.add, op1=ALU.mult))
            m2 = V.did(V.e.scalar_tensor_tensor(out=PT_[0][:, :, :], in0=g3, scalar=1.0, in1=maskn(upper[:, 0, :]), op0=ALU.add, op1=ALU.mult))
            banks.done(i, m2)
            V.wait(m2)
            my = V.did(V.e.tensor_tensor(Y[:, bs, :], maskn(ident[:, :]), PT_[0][:, :, :], ALU.subtract))
            i, ps = banks.take(PE)
            for c in range(TPB):
                cs = slice(c * P, (c + 1) * P)
                last = PE.e.matmul(ps[:, cs], kT[:, b, cs], qT[:, b, cs], start=True, stop=True)
            m = PE.did(last)
            V.wait(m)
            m = V.did(V.e.scalar_tensor_tensor(out=nat[:, bs, :], in0=ps.rearrange("p (c t) -> p c t", c=TPB), scalar=1.0,
                                               in1=maskn(upper[:, 1, :]), op0=ALU.add, op1=ALU.mult))
            banks.done(i, m)
            for j in range(6):
                n0, t0, n1, t1 = PN[j % 2], PT_[j % 2], PN[(j + 1) % 2], PT_[(j + 1) % 2]
                PE.wait(m1, m2)
                i, ps = banks.take(PE)
                for c in range(TPB):
                    last = PE.e.matmul(ps[:, c * P:(c + 1) * P], t0[:, c, :], n0[:, c, :], start=True, stop=True)
                m = PE.did(last)
                A.wait(m, my)
                m1n = A.did(A.e.activation(n1[:, :, :].rearrange("p c t -> p (c t)"), ps, ACT.Copy))
                banks.done(i, m1n)
                if j < 5:
                    i, ps = banks.take(PE)
                    for c in range(TPB):
                        last = PE.e.matmul(ps[:, c * P:(c + 1) * P], n0[:, c, :], t0[:, c, :], start=True, stop=True)
                    m = PE.did(last)
                    V.wait(m)
                    m2 = V.did(V.e.tensor_copy(t1[:, :, :].rearrange("p c t -> p (c t)"), ps))
                    banks.done(i, m2)
                m1 = m1n
                i, ps = banks.take(PE)
                PE.wait(m1, my)
                for c in range(TPB):
                    last = PE.e.matmul(ps[:, c * P:(c + 1) * P], n1[:, c, :], Y[:, b * TPB + c, :], start=True, stop=True)
                m = PE.did(last)
                V.wait(m)
                my = V.did(V.e.tensor_tensor(Y[:, bs, :], Y[:, bs, :], ps.rearrange("p (c t) -> p c t", c=TPB), ALU.add))
                banks.done(i, my)
            pn_free = m
            y_marks.append(my)

        w_mark, b_mark, u_free = theta_mark, loaded, None
        PE.wait(*ktok_marks, *y_marks)
        for c in range(TPB):
            cs = slice(c * P, (c + 1) * P)
            PE.wait(w_mark, b_mark)
            i, ps = banks.take(PE)
            for b in range(B):
                o = ps[:, b * P:(b + 1) * P]
                PE.e.matmul(o, kT[:, b, cs], WT[:, b, :], start=True, stop=False)
                PE.e.matmul(o, ones[0:1, :], brow[:, b, :], start=False, stop=False)
                last = PE.e.matmul(o, hT[:, b, cs], thetaT[:, 1, :], start=False, stop=True)
            m = PE.did(last)
            A.wait(m, u_free)
            r_mark = A.did(A.e.activation(R[:, :, :].rearrange("p b d -> p (b d)"), ps, ACT.Copy))
            banks.done(i, r_mark)
            i, ps = banks.take(PE)
            PE.wait(r_mark)
            for b in range(B):
                last = PE.e.matmul(ps[:, b * P:(b + 1) * P], Y[:, b * TPB + c, :], R[:, b, :], start=True, stop=True)
            m = PE.did(last)
            A.wait(m)
            u_mark = A.did(A.e.activation(U[:, :, :].rearrange("p b d -> p (b d)"), ps, ACT.Copy))
            banks.done(i, u_mark)
            i, ps = banks.take(PE)
            PE.wait(u_mark)
            for b in range(B):
                o = ps[:, b * P:(b + 1) * P]
                PE.e.matmul(o, WT[:, b, :], qT[:, b, cs], start=True, stop=False)
                PE.e.matmul(o, brow[:, b, :], ones[0:1, :], start=False, stop=False)
                last = PE.e.matmul(o, U[:, b, :], nat[:, b * TPB + c, :], start=False, stop=True)
            m = PE.did(last)
            V.wait(m)
            for b in range(B):
                x_mark = V.did(V.e.scalar_tensor_tensor(out=xT[:, b, cs], in0=ps[:, b * P:(b + 1) * P], scalar=gate[:, 0, 0, b:b + 1],
                                                        in1=xT[:, b, cs], op0=ALU.mult, op1=ALU.add))
            banks.done(i, x_mark)
            if c == TPB - 1:
                break
            i, ps = banks.take(PE)
            for b in range(B):
                last = PE.e.matmul(ps[:, b * P:(b + 1) * P], ktok[:, b * TPB + c, :], U[:, b, :], start=True, stop=True)
            m = PE.did(last)
            V.wait(m)
            w_mark = V.did(V.e.scalar_tensor_tensor(out=WT[:, :, :].rearrange("p b d -> p (b d)"), in0=ps, scalar=-ETA,
                                                    in1=WT[:, :, :].rearrange("p b d -> p (b d)"), op0=ALU.mult, op1=ALU.add))
            banks.done(i, w_mark)
            i, ps = banks.take(PE)
            for b in range(B):
                last = PE.e.matmul(ps[0:1, b * P:(b + 1) * P], ones[:, 0:1], U[:, b, :], start=True, stop=True)
            u_free = PE.did(last)
            V.wait(u_free)
            b_mark = V.did(V.e.scalar_tensor_tensor(out=brow[:, :, :].rearrange("p b d -> p (b d)"), in0=ps[0:1, :], scalar=-ETA,
                                                    in1=brow[:, :, :].rearrange("p b d -> p (b d)"), op0=ALU.mult, op1=ALU.add))
            banks.done(i, b_mark)
    meet()
    transformer(core)
    meet()
    relative_attention(core)
    meet()
    experts(core)
    meet()

    with ExitStack() as scope:
        ytok = sbuf(scope, "ytok", [P, NT, P])
        stored = Loads(nc, "stored")
        out = io["out"].rearrange("b (c p) d -> p (b c) d", p=P)
        for b in range(B):
            i, ps = banks.take(PE)
            for c in range(TPB):
                last = PE.e.transpose(ps[:, c * P:(c + 1) * P], xT[:, b, c * P:(c + 1) * P], ident[:, :])
            m = PE.did(last)
            A.wait(m)
            m = A.did(A.e.activation(ytok[:, b * TPB:(b + 1) * TPB, :].rearrange("p c d -> p (c d)"), ps, ACT.Copy))
            banks.done(i, m)
            SP.wait(m)
            stored.start(SP, out[:, b * TPB:(b + 1) * TPB, :], ytok[:, b * TPB:(b + 1) * TPB, :])
        SP.wait(stored.mark())


def transformer(core):
    io, PE, V, A, G, SP, banks = core.io, core.PE, core.V, core.A, core.G, core.SP, core.banks
    ident, ones, xT, modT, gate = core.ident, core.ones, core.xT, core.modT, core.gate
    with ExitStack() as scope:
        def sb(name, shape, dt=F32):
            return core.sbuf(scope, name, shape, dt)

        z = sb("z", [P, B, S])
        xh, xl = (sb(n, [P, B, S], F32R) for n in ("xs_high", "xs_low"))
        w_raw = sb("wqkv", [P, 3 * INNER])
        wh, wl = (sb(n, [P, 3 * INNER], F32R) for n in ("wqkv_high", "wqkv_low"))
        wo = [sb(f"wo{i}", [P, PAIRS, P]) for i in range(2)]
        w1 = [sb(f"w1_{i}", [P, 2 * DI]) for i in range(2)]
        w2 = [sb(f"w2_{i}", [P, 3, P]) for i in range(2)]
        cols = sb("cols", [P, 3, DEPTH])
        b1c = sb("b1c", [P, 2, 3, DEPTH])
        rot = [sb(f"rot{i}", [P, 4, TPB, DH]) for i in range(2)]
        scales = sb("scales", [P, 2, DEPTH, DH])
        maskb = sb("maskb", [P, 2, 2, KB], BF16)
        ss = Ring([sb(f"ss{i}", [P, 3, 2 * HEADS]) for i in range(2)])
        swap_ring = Ring([sb(f"swap{i}", [P, 512]) for i in range(2)])
        xc_ring = Ring([sb("xc", [P, S])])
        act = sb("act", [P, 3, S])
        act_ring = Ring([act])
        rows = act[0:1, 0:2, 0:DEPTH * DH].rearrange("a j (l d) -> a j l d", d=DH)
        mask = act[:, 2, 0:2 * KB].rearrange("p (j k) -> p j k", j=2)
        a_ring = Ring([sb(f"qk{i}", [P, 2 * INNER]) for i in range(2)])
        q_ring = Ring([sb(f"qT{i}", [P, PAIRS, 2, P]) for i in range(2)])
        k_ring = Ring([sb(f"kT{i}", [P, PAIRS, WIN + P]) for i in range(2)])
        vt_ring = Ring([sb(f"v_tok{i}", [P, INNER]) for i in range(2)])
        v_ring = Ring([sb(f"v_win{i}", [KB, 2, INNER]) for i in range(2)])
        v_loads = [Loads(core.nc, f"v_windows{i}") for i in range(2)]
        p_ring = Ring([sb(f"p{i}", [P, PAIRS, 2, KB]) for i in range(2)])
        stat_ring = Ring([sb(f"stat{i}", [P, 3, HEADS]) for i in range(2)])
        pt_ring = Ring([sb(f"pT{i}", [KB, 2, 2, P]) for i in range(2)])
        o_ring = Ring([sb(f"oT{i}", [P, PAIRS, P]) for i in range(2)])

        raw_loads = Loads(core.nc, "wqkv_load")
        raw_loaded, split_mark = {0: raw_loads.start(SP, w_raw[:, :], io["L0_ffn_Wqkv"][0])}, {}
        once = Loads(core.nc, "ffn_once")
        once.start(SP, mask[:, :, :], io["c_mask"])
        for j, n in enumerate(("ln_g", "ln_b", "b2")):
            once.start(SP, cols[:, j, :], io["L0_ffn_" + n].rearrange("l d -> d l"))
        for half in range(2):
            for j, (lo, n) in enumerate(CHUNKS):
                once.start(SP, b1c[0:n, half, j, :], io["L0_ffn_b1"][:, half * DI + lo:half * DI + lo + n].rearrange("l d -> d l"))
        for j, n in enumerate(("q_scale", "k_scale")):
            once.start(SP, rows[:, j, :, :], io["L0_ffn_" + n].rearrange("(a l) d -> a l d", a=1))
        weights = [Loads(core.nc, f"ffn_weights{i}") for i in range(2)]
        rot_loads = [Loads(core.nc, f"rot_loads{i}") for i in range(2)]

        def load_layer(l, *free):
            SP.wait(*free)
            w = weights[l % 2]
            w.start(SP, wo[l % 2][:, :, :], io["L0_ffn_Wo"][l].rearrange("(h p) d -> p h d", p=P))
            w.start(SP, w1[l % 2][:, :], io["L0_ffn_W1"][l])
            for j, (lo, n) in enumerate(CHUNKS):
                m = w.start(SP, w2[l % 2][0:n, j, :], io["L0_ffn_W2"][l, lo:lo + n, :])
            return m

        layer_loaded = {0: load_layer(0)}

        def split_weights(l, u, *free):
            cs = slice(u * 512, (u + 1) * 512)
            A.wait(raw_loaded[l], *free)
            m = A.did(A.e.activation(wh[:, cs], w_raw[:, cs], ACT.Copy))
            en = G if l else V
            en.wait(m)
            split_mark[l, u] = m = en.did(en.e.tensor_tensor(wl[:, cs], w_raw[:, cs], wh[:, cs].bitcast(F32), ALU.subtract))
            if u == 5 and l + 1 < DEPTH:
                SP.wait(m)
                raw_loaded[l + 1] = raw_loads.start(SP, w_raw[:, :], io["L0_ffn_Wqkv"][l + 1])

        G.did(G.e.memset(xh[:, :, :].bitcast(F32), 0.0))
        zero = G.did(G.e.memset(xl[:, :, :].bitcast(F32), 0.0))
        for q in q_ring.buffers:
            zero = G.did(G.e.memset(q[:, :, :, :], 0.0))
        A.wait(zero)
        V.wait(once.mark())
        V.did(V.e.tensor_copy(maskb[:, 0, 0, :], mask[:, 1, :]))
        V.did(V.e.tensor_copy(maskb[:, 0, 1, :], mask[:, 0, :]))
        V.did(V.e.tensor_copy(maskb[:, 1, :, :], mask[:, 0, :].unsqueeze(1).to_broadcast([P, 2, KB])))
        V.did(V.e.tensor_copy(core.center_r[:, :], core.center[:, :]))
        mask_mark = V.did(V.e.tensor_copy(core.identb[:, :], ident[:, :]))

        PE.wait(once.mark())
        for j in range(2):
            i, ps = banks.take(PE)
            m = PE.did(PE.e.matmul(ps[:, 0:DEPTH * DH], ones[0:1, :], rows[:, j, :, :].rearrange("a l d -> a (l d)"), start=True, stop=True))
            A.wait(m)
            scales_mark = A.did(A.e.activation(scales[:, j, :, :].rearrange("p l d -> p (l d)"), ps[:, 0:DEPTH * DH], ACT.Copy))
            banks.done(i, scales_mark)

        def rotary_tables(l, *free):
            SP.wait(*free)
            G.wait(scales_mark, rot_loads[l % 2].start(SP, rot[l % 2][:, :, :, :], io["c_rot"]))
            for j in range(2):
                plain = scales[:, j, l, :].unsqueeze(1).to_broadcast([P, TPB, DH])
                swapped = scales[:, j, l, :].rearrange("p (a e) -> p a e", a=2)[:, ::-1, :]
                even, odd = rot[l % 2][:, 2 * j, :, :], rot[l % 2][:, 2 * j + 1, :, :]
                G.did(G.e.tensor_tensor(even, even, plain, ALU.mult))
                for c in range(TPB):
                    one = odd[:, c, :].rearrange("p (a e) -> p a e", a=2)
                    m = G.did(G.e.tensor_tensor(one, one, swapped, ALU.mult))
            return m

        def shift(b, *marks):
            for en in (A, V, G):
                en.wait(zero, *marks)
            h = P // 2
            G.wait(A.did(A.e.activation(xh[0:h, b, :], z[0:h, b, :], ACT.Copy)))
            V.wait(V.did(V.e.tensor_copy(xh[h:P, b, 1:S], z[h:P, b, 0:S - 1])))
            return (G.did(G.e.tensor_tensor(xl[0:h, b, :], z[0:h, b, :], xh[0:h, b, :].bitcast(F32), ALU.subtract)),
                    V.did(V.e.tensor_tensor(xl[h:P, b, 1:S], z[h:P, b, 0:S - 1], xh[h:P, b, 1:S].bitcast(F32), ALU.subtract)))

        PERIOD = 8
        keys, window_mark, vt_of, v_window, xs_read, z_done, ffn_done = {}, {}, {}, {}, {}, {}, {}

        def tile(l, t):
            b, c = divmod(t, TPB)
            tab = rot[l % 2]
            high, low = (x[:, b, c * P:(c + 1) * P] for x in (xh, xl))
            si, s2 = ss.take(V)
            ai, a = a_ring.take(V)
            held, squared, held_v, used = {}, {}, {}, {}

            def product(ps, u):
                cs = slice(u * 512, (u + 1) * 512)
                PE.wait(split_mark[l, u])
                PE.e.matmul(ps, high, wl[:, cs], start=True, stop=False)
                PE.e.matmul(ps, low, wh[:, cs], start=False, stop=False)
                m = PE.did(PE.e.matmul(ps, high, wh[:, cs], start=False, stop=True))
                if t == NT - 1:
                    used[u] = m
                return m

            def split_next(u):
                if t == NT - 1 and l + 1 < DEPTH:
                    split_weights(l + 1, u, used[u])

            def project(u):
                i, ps = banks.take(PE)
                held[u] = (i, ps, product(ps, u))

            def square(u):
                i, ps, m = held[u]
                qi, sq = core.sq_ring.take(A)
                A.wait(m)
                squared[u] = (qi, sq, A.did(A.e.activation(sq[:, :], ps, ACT.Square)))

            def rotate(u):
                (i, ps, _), (qi, sq, m) = held[u], squared[u]
                part, j = slice(u * 512, (u + 1) * 512), u // 2
                bi, s = swap_ring.take(V)
                V.wait(m)
                m = V.did(V.e.tensor_reduce(s2[:, 0, u * 8:(u + 1) * 8], sq[:, :].rearrange("p (h e) -> p h e", e=DH), AX, ALU.add))
                core.sq_ring.done(qi, m)
                p3, a3, s3 = (x.rearrange("p (h e) -> p h e", e=DH) for x in (ps, a[:, part], s[:, :]))
                V.did(V.e.tensor_tensor(a3, p3, tab[:, 2 * j, c, :].unsqueeze(1).to_broadcast([P, 8, DH]), ALU.mult))
                for half in range(2):
                    to, of = half * 32, (1 - half) * 32
                    m = V.did(V.e.tensor_tensor(s3[:, :, to:to + 32], p3[:, :, of:of + 32],
                                                tab[:, 2 * j + 1, c, to:to + 32].unsqueeze(1).to_broadcast([P, 8, 32]), ALU.mult))
                banks.done(i, m)
                G.wait(m)
                m = G.did(G.e.tensor_tensor(a[:, part], a[:, part], s[:, :], ALU.add))
                swap_ring.done(bi, m)
                return m

            def scale(u, *marks):
                V.wait(*marks)
                a3 = a[:, u * 512:(u + 1) * 512].rearrange("p (h e) -> p h e", e=DH)
                return V.did(V.e.tensor_tensor(a3, a3, s2[:, 1, u * 8:(u + 1) * 8].unsqueeze(2).to_broadcast([P, 8, DH]), ALU.mult))

            def turn(g, *marks):
                i, ps = banks.take(PE)
                PE.wait(*marks)
                for e in range(4):
                    at = (g * 4 + e) * P
                    last = PE.e.transpose(ps[:, e * P:(e + 1) * P], a[:, at:at + P], ident[:, :])
                held[g] = (i, ps, PE.did(last))

            def keep(g, q, k):
                i, ps, m = held[g]
                A.wait(m)
                n = g % 2 * 4
                if g < 2:
                    for f in range(2):
                        fs = slice(f * DH, (f + 1) * DH)
                        m = A.did(A.e.activation(q[fs, n:n + 4, :, fs], ps[fs, :].rearrange("p (h u t) -> p h u t", h=4, u=2), ACT.Copy))
                else:
                    m = A.did(A.e.activation(k[:, n:n + 4, WIN:WIN + P], ps.rearrange("p (h t) -> p h t", h=4), ACT.Copy))
                banks.done(i, m)
                return m

            def values(half):
                i, ps = banks.take(PE)
                m = xs_read[b] = product(ps, 4 + half)
                held_v[half] = (i, ps, m)

            def keep_values(half, vt):
                i, ps, m = held_v[half]
                A.wait(m)
                m = A.did(A.e.activation(vt[:, half * 512:(half + 1) * 512], ps, ACT.Copy))
                banks.done(i, m)
                return m

            def windows(vi, v, vt, mark):
                load = v_loads[vi]
                SP.wait(mark)
                if c == 0:
                    zeros = G.did(G.e.memset(v[0:WIN, 0, :], 0.0))
                else:
                    zeros = None
                    load.start(SP, v[0:WIN, 0, :], vt_of[l, t - 1][P - WIN:P, :])
                load.start(SP, v[WIN:KB, 0, :], vt[0:QB, :])
                m = v_window[l, t] = load.start(SP, v[:, 1, :], vt[QB - WIN:P, :])
                return m, zeros

            PE.wait(layer_loaded[l], *xs_marks[b])
            project(0)
            yield
            project(1)
            square(0)
            V.wait(tables[l])
            yield
            rotate(0)
            project(2)
            square(1)
            split_next(0)
            yield
            rotate(1)
            project(3)
            square(2)
            split_next(1)
            yield
            rotate(2)
            square(3)
            split_next(2)
            yield
            rotated = rotate(3)
            split_next(3)
            yield
            V.wait(V.last())
            m = V.did(V.e.tensor_scalar(s2[:, 0, :], s2[:, 0, :], 1e-24, None, ALU.max))
            root = core.inverse_root(s2[:, 1, :], s2[:, 0, :], s2[:, 2, :], m, V)
            yield
            yield
            scale(0, root, rotated)
            scaled_q = scale(1)
            yield
            turn(0, scaled_q)
            scale(2)
            scaled = scale(3)
            ss.done(si, scaled)
            yield
            qi, q = q_ring.take(A)
            ki, k = k_ring.take(A, G)
            keep(0, q, k)
            turn(1)
            yield
            if c == 0:
                km = G.did(G.e.memset(k[:, :, 0:WIN], 0.0))
            else:
                before, before_mark = keys[l, t - 1]
                G.wait(before_mark)
                km = G.did(G.e.tensor_copy(k[:, :, 0:WIN], before[:, :, P:P + WIN]))
            window_mark[l, t] = km
            keep(1, q, k)
            turn(2, scaled)
            values(0)
            yield
            wi, vt = vt_ring.take(A)
            vt_of[l, t] = vt
            keep(2, q, k)
            turn(3)
            a_ring.done(ai, PE.last())
            keep_values(0, vt)
            split_next(4)
            yield
            k_mark = keep(3, q, k)
            keys[l, t] = (k, k_mark)
            values(1)
            yield

            pi, p = p_ring.take(A, G)
            xi, stat = stat_ring.take(V, A)
            mk = maskb[:, 0 if c == 0 else 1, :, :]
            scored, stats, turned, sums = {}, {}, {}, {}

            def scores(g):
                i, ps = banks.take(PE)
                PE.e.matmul(ps[:, 0:4 * KB].rearrange("p (h n) -> p h n", h=2), core.identb[:, :],
                            mk.rearrange("p u n -> p (u n)").unsqueeze(1).to_broadcast([P, 2, 2 * KB]), start=True, stop=False)
                for j in range(2):
                    for u in range(2):
                        at = (2 * j + u) * KB
                        last = PE.e.matmul(ps[:, at:at + KB], q[:, 2 * g + j, u, :], k[:, 2 * g + j, u * QB:u * QB + KB],
                                           start=False, stop=(j == 1 and u == 1))
                scored[g] = (i, ps, PE.did(last))

            def largest(g):
                i, ps, m = scored[g]
                V.wait(m)
                stats[g] = V.did(V.e.tensor_reduce(stat[:, 0, 4 * g:4 * g + 4], ps[:, 0:4 * KB].rearrange("p (n k) -> p n k", n=4), AX, ALU.max,
                                                   negate=True))

            def exponentials(g):
                i, ps, _ = scored[g]
                A.wait(stats[g])
                for n in range(4):
                    h = 4 * g + n
                    m = A.did(A.e.activation(p[:, 2 * g + n // 2, n % 2, :], ps[:, n * KB:(n + 1) * KB], ACT.Exp, bias=stat[:, 0, h:h + 1],
                                             accum_out=stat[:, 1, h:h + 1]))
                banks.done(i, m)
                stats[g] = m

            def normalise(g):
                four = slice(4 * g, 4 * g + 4)
                V.wait(stats[g])
                m = V.did(V.e.reciprocal(stat[:, 2, four], stat[:, 1, four]))
                G.wait(m)
                p4 = p[:, 2 * g:2 * g + 2, :, :].rearrange("p h u k -> p (h u) k")
                stats[g] = G.did(G.e.tensor_tensor(p4, p4, stat[:, 2, four].unsqueeze(2).to_broadcast([P, 4, KB]), ALU.mult))

            def by_key(g):
                i, ps = banks.take(PE)
                PE.wait(stats[g])
                for j in range(2):
                    for u in range(2):
                        last = PE.e.transpose(ps[0:KB, (2 * j + u) * P:(2 * j + u + 1) * P], p[:, 2 * g + j, u, :], ident[:, :])
                turned[g] = (i, ps, PE.did(last))

            def keep_by_key(g):
                i, ps, m = turned[g]
                ti, pt = pt_ring.take(A)
                A.wait(m)
                m = A.did(A.e.activation(pt[:, :, :, :].rearrange("k h u q -> k (h u q)"), ps[0:KB, :], ACT.Copy))
                banks.done(i, m)
                turned[g] = (ti, pt, m)

            def weighted(g, *marks):
                ti, pt, m = turned[g]
                PE.wait(m, *marks)
                if g % 2 == 0:
                    sums["bank"] = banks.take(PE)
                for j in range(2):
                    for f in range(2):
                        h, fs = 2 * (2 * g + j) + f, slice(f * DH, (f + 1) * DH)
                        for u in range(2):
                            at = (g % 2 * 2 + j) * P + u * QB
                            last = PE.e.matmul(sums["bank"][1][fs, at:at + QB], v[:, u, h * DH:(h + 1) * DH], pt[:, j, u, fs], start=True, stop=True)
                m = sums["mark"] = PE.did(last)
                pt_ring.done(ti, m)

            def keep_weighted(g):
                i, ps = sums["bank"]
                A.wait(sums["mark"])
                m = A.did(A.e.activation(o[:, 2 * g - 2:2 * g + 2, :], ps.rearrange("p (h t) -> p h t", h=4), ACT.Copy))
                banks.done(i, m)
                return m

            PE.wait(k_mark, km, mask_mark)
            scores(0)
            vi, v = v_ring.take(SP, G)
            v_marks = windows(vi, v, vt, keep_values(1, vt))
            split_next(5)
            yield
            largest(0)
            yield
            exponentials(0)
            scores(1)
            yield
            normalise(0)
            largest(1)
            yield
            exponentials(1)
            scores(2)
            yield
            normalise(1)
            largest(2)
            yield
            exponentials(2)
            scores(3)
            by_key(0)
            q_ring.done(qi, scored[3][2])
            yield
            k_ring.done(ki, scored[3][2], window_mark[l, t + 1] if c < TPB - 1 else None)
            normalise(2)
            largest(3)
            keep_by_key(0)
            yield
            exponentials(3)
            by_key(1)
            weighted(0, *v_marks)
            yield
            normalise(3)
            vt_ring.done(wi, v_marks[0], v_window[l, t + 1] if c < TPB - 1 else None)
            stat_ring.done(xi, stats[3])
            keep_by_key(1)
            yield
            by_key(2)
            weighted(1)
            yield
            keep_by_key(2)
            oi, o = o_ring.take(A)
            keep_weighted(1)
            yield
            by_key(3)
            p_ring.done(pi, PE.last())
            weighted(2)
            yield
            keep_by_key(3)
            yield
            weighted(3)
            v_ring.done(vi, PE.last())
            yield
            o_mark = keep_weighted(3)
            yield
            i, ps = banks.take(PE)
            PE.wait(o_mark)
            for h in range(PAIRS):
                last = PE.e.matmul(ps[:, 0:P], wo[l % 2][:, h, :], o[:, h, :], start=(h == 0), stop=(h == PAIRS - 1))
            m = PE.did(last)
            o_ring.done(oi, m)
            yield
            zt = z[:, b, c * P:(c + 1) * P]
            V.wait(m)
            m = V.did(V.e.tensor_tensor(zt, zt, ps[:, 0:P], ALU.add))
            banks.done(i, m)
            z_done[l, b] = m

        def feed_forward(l, b):
            yield
            xs_marks[b] = shift(b, z_done[l, b], xs_read[b])
            ci, x = xc_ring.take(A)
            x = x[:, :]
            yield
            n_mark = yield from core.layer_norm_steps(x, (xh[:, b, :], xl[:, b, :]), x, cols[:, 0, l:l + 1], cols[:, 1, l:l + 1], b, *xs_marks[b])
            yield
            w = w1[l % 2]
            ai, act = act_ring.take(A, V)
            while len(banks.idle) < 4:
                yield
            PE.wait(n_mark)
            gates = []
            for lo, n in CHUNKS:
                i, ps = banks.take(PE)
                gates.append((i, ps, PE.did(PE.e.matmul(ps[0:n, :], w[:, DI + lo:DI + lo + n], x, start=True, stop=True))))
            yield
            for j, (lo, n) in enumerate(CHUNKS):
                i, ps, m = gates[j]
                A.wait(m)
                g_mark = A.did(A.e.activation(act[0:n, j, :], ps[0:n, :], ACT.Gelu, bias=b1c[0:n, 1, j, l:l + 1]))
                banks.done(i, g_mark)
            for j, (lo, n) in enumerate(CHUNKS):
                i, ps = banks.take(PE)
                m = PE.did(PE.e.matmul(ps[0:n, :], w[:, lo:lo + n], x, start=True, stop=True))
                yield
                V.wait(m, g_mark)
                m = V.did(V.e.scalar_tensor_tensor(out=act[0:n, j, :], in0=ps[0:n, :], scalar=b1c[0:n, 0, j, l:l + 1],
                                                   in1=act[0:n, j, :], op0=ALU.add, op1=ALU.mult))
                banks.done(i, m)
            xc_ring.done(ci, PE.last())
            yield
            i, ps = banks.take(PE)
            PE.wait(m)
            for j, (lo, n) in enumerate(CHUNKS):
                last = PE.e.matmul(ps, w2[l % 2][0:n, j, :], act[0:n, j, :], start=(j == 0), stop=(j == 2))
            m = PE.did(last)
            act_ring.done(ai, m)
            yield
            V.wait(m)
            m = V.did(V.e.scalar_tensor_tensor(out=z[:, b, :], in0=ps, scalar=cols[:, 2, l:l + 1], in1=z[:, b, :], op0=ALU.add, op1=ALU.add))
            banks.done(i, m)
            yield
            if l + 1 < DEPTH:
                xs_marks[b] = shift(b, m)
            else:
                V.wait(m)
                V.did(V.e.scalar_tensor_tensor(out=xT[:, b, :], in0=z[:, b, :], scalar=gate[:, 0, 1, b:b + 1], in1=xT[:, b, :],
                                               op0=ALU.mult, op1=ALU.add))
            ffn_done[l, b] = True

        tables = {0: rotary_tables(0)}
        z_marks = core.side_by_side([core.layer_norm_steps(z[:, b, :], xT[:, b, :], z[:, b, :], modT[:, 0, 4, b:b + 1],
                                                           modT[:, 0, 3, b:b + 1], b) for b in range(B)])
        xs_marks = [shift(b, z_marks[b]) for b in range(B)]
        for u in range(6):
            split_weights(0, u)

        waiting = [(l, t) for l in range(DEPTH) for t in range(NT)]
        running, since = [], PERIOD
        while waiting or running:
            if waiting and since >= PERIOD:
                l, t = waiting[0]
                if l == 0 or (l - 1, t // TPB) in ffn_done:
                    running.append((waiting.pop(0), tile(l, t)))
                    since = 0
                    if t == NT - TPB and l + 1 < DEPTH:
                        layer_loaded[l + 1] = load_layer(l + 1, PE.last())
                        tables[l + 1] = rotary_tables(l + 1, V.last())
            since += 1
            for name, steps in list(running):
                if next(steps, "end") == "end":
                    running = [r for r in running if r[0] != name]
                    if len(name) == 2 and name[1] % TPB == TPB - 1:
                        running.append(((*name, "ffn"), feed_forward(name[0], name[1] // TPB)))


def relative_attention(core):
    nc, io, PE, V, A, G, SP, banks = core.nc, core.io, core.PE, core.V, core.A, core.G, core.SP, core.banks
    ident, ones, xT, modT, gate = core.ident, core.ones, core.xT, core.modT, core.gate
    copy, isq = ACT.Copy, float(D2) ** -0.5
    mid = EXT // 2
    table_rows = 2 * M2 + 1
    q_dram, k_dram = (core.scratch(n, [H2, 3, D2, B * S], BF16) for n in ("q_parts", "k_parts"))
    rk_dram = core.scratch("rel_k_parts", [3, D2, ROW], BF16)
    rv_dram = core.scratch("rel_v_ext", [ROW, D2])
    HG, UB, NR = 2, 2, 4
    qr_dram = core.scratch("by_position", [SLOTS, HG, P, ROW])
    o_dram = core.scratch("rel_values", [TPB * B // UB, D2, P // NR, NR, UB * H2])

    with ExitStack() as scope:
        def sb(name, shape, dt=F32):
            return core.sbuf(scope, name, shape, dt)

        vt = sb("v_tok", [P, NT, P])
        v_ends = sb("v_ends", [P, 2, P])
        woT = sb("woT2", [P, P])
        colb = sb("col_bias", [P, 4])
        rk = sb("rk", [KS, ROW], BF16)
        tv = sb("rel_v_window", [P, 3 * P, D2])
        once = Loads(nc, "rel_once")
        for j, n in enumerate(("bq", "bk", "bo")):
            once.start(SP, colb[:, j:j + 1], io["L1_attn_" + n].rearrange("(d a) -> d a", a=1))
        ext = Loads(nc, "rel_v_store")
        rel_v = io["L1_attn_rel_v"]
        ext.start(SP, rv_dram[mid - M2:mid + M2 + 1, :], rel_v)
        ext.start(SP, rv_dram[0:mid - M2, :], rel_v[0:1, :].to_broadcast([mid - M2, D2]))
        ext.start(SP, rv_dram[mid + M2 + 1:ROW, :], rel_v[table_rows - 1:table_rows, :].to_broadcast([ROW - mid - M2 - 1, D2]))

        with ExitStack() as early:
            def se(name, shape, dt=F32):
                return core.sbuf(early, name, shape, dt)

            wraw = se("w_raw", [P, 4, P])
            wT = se("wT2", [P, 3, P])
            hT, xc = se("hT2", [P, B, S]), se("xc2", [P, B, S])
            brow, evrow = se("bv_row", [1, P]), se("end_rows", [1, 2, D2])
            rkf = se("rkf", [D2, 2, ROW])
            part_ring = Ring([se(f"part{i}", [P, 2, S]) for i in range(2)])
            bf_ring = Ring([se(f"bf{i}", [P, 3, S], BF16) for i in range(2)])
            rkb = se("rkb", [D2, 3, ROW], BF16)
            for j, n in enumerate(("Wq", "Wk", "Wv", "Wo")):
                once.start(SP, wraw[:, j, :], io["L1_attn_" + n])
            once.start(SP, brow[:, :], io["L1_attn_bv"].rearrange("(a d) -> a d", a=1))
            once.start(SP, evrow[:, 0, :], rel_v[0:1, :])
            once.start(SP, evrow[:, 1, :], rel_v[table_rows - 1:table_rows, :])
            once.start(SP, rkf[:, 0, mid - M2:mid + M2 + 1], io["L1_attn_rel_k"].rearrange("t d -> d t"))
            loaded = once.mark()
            windows = Loads(nc, "rel_v_windows")
            SP.wait(ext.mark())
            tv_mark = windows.start(SP, tv[:, :, :], bass.AP(rv_dram.tensor, 0, [[D2, P], [D2, 3 * P], [1, D2]]))

            h_marks = core.side_by_side([core.layer_norm_steps(hT[:, b, :], xT[:, b, :], xc[:, b, :], modT[:, 1, 1, b:b + 1],
                                                               modT[:, 1, 0, b:b + 1], b) for b in range(B)])
            i, ps = banks.take(PE)
            PE.wait(loaded)
            for j in range(4):
                last = PE.e.transpose(ps[:, j * P:(j + 1) * P], wraw[:, j, :], ident[:, :])
            m = PE.did(last)
            V.wait(m)
            V.did(V.e.tensor_copy(wT[:, :, :].rearrange("p j d -> p (j d)"), ps[:, 0:3 * P]))
            w_mark = V.did(V.e.tensor_copy(woT[:, :], ps[:, 3 * P:4 * P]))
            banks.done(i, w_mark)
            i, ps = banks.take(PE)
            for j in range(2):
                last = PE.e.matmul(ps[:, j * D2:(j + 1) * D2], ones[0:1, :], evrow[:, j, :], start=True, stop=True)
            m = PE.did(last)
            V.wait(m)
            ends_mark = V.did(V.e.tensor_copy(v_ends[:, :, :].rearrange("p j (h d) -> p j h d", d=D2),
                                              ps[:, 0:2 * D2].rearrange("p (j d) -> p j d", j=2).unsqueeze(2).to_broadcast([P, 2, H2, D2])))
            banks.done(i, ends_mark)

            V.wait(loaded)
            lo, hi = mid - M2, mid + M2
            V.did(V.e.tensor_copy(rkf[:, 0, 0:lo], rkf[:, 0, lo:lo + 1].to_broadcast([D2, lo])))
            m = V.did(V.e.tensor_copy(rkf[:, 0, hi + 1:ROW], rkf[:, 0, hi:hi + 1].to_broadcast([D2, ROW - hi - 1])))
            V.wait(m)
            m = V.did(V.e.tensor_copy(rkb[:, 0, :], rkf[:, 0, :]))
            for j in range(2):
                V.wait(m)
                m = V.did(V.e.tensor_tensor(rkf[:, 1 - j, :], rkf[:, j, :], rkb[:, j, :], ALU.subtract))
                V.wait(m)
                m = V.did(V.e.tensor_copy(rkb[:, j + 1, :], rkf[:, 1 - j, :]))
            parts = [Loads(nc, f"parts_store{i}") for i in range(3)]
            SP.wait(m)
            SP.wait(parts[2].start(SP, rk_dram.rearrange("r d t -> d r t"), rkb[:, :, :]))
            rk_loads = Loads(nc, "rk_loads")
            for r in range(3):
                rk_mark = rk_loads.start(SP, rk[r * 3 * D2:(r + 1) * 3 * D2, :], rk_dram[r].unsqueeze(0).to_broadcast([3, D2, ROW]))

            PE.wait(w_mark)
            for b in range(B):
                PE.wait(h_marks[b])
                for j, dram in ((0, q_dram), (1, k_dram)):
                    i, ps = banks.take(PE)
                    m = PE.did(PE.e.matmul(ps, wT[:, j, :], hT[:, b, :], start=True, stop=True))
                    xi, part = part_ring.take(A, V)
                    bi, bf = bf_ring.take(V)
                    A.wait(m, loaded)
                    m = A.did(A.e.activation(part[:, 0, :], ps, ACT.Identity, bias=colb[:, j:j + 1]))
                    banks.done(i, m)
                    V.wait(m)
                    m = V.did(V.e.tensor_copy(bf[:, 0, :], part[:, 0, :]))
                    for r in range(2):
                        V.wait(m)
                        m = V.did(V.e.tensor_tensor(part[:, 1 - r, :], part[:, r, :], bf[:, r, :], ALU.subtract))
                        V.wait(m)
                        m = V.did(V.e.tensor_copy(bf[:, r + 1, :], part[:, 1 - r, :]))
                    part_ring.done(xi, m)
                    SP.wait(m)
                    for r in range(3):
                        stored = parts[bi].start(SP, dram[:, r, :, b * S:(b + 1) * S], bf[:, r, :])
                    bf_ring.done(bi, stored)
                i, ps = banks.take(PE)
                for c in range(TPB):
                    o = ps[:, c * P:(c + 1) * P]
                    PE.e.matmul(o, hT[:, b, c * P:(c + 1) * P], wT[:, 2, :], start=True, stop=False)
                    last = PE.e.matmul(o, ones[0:1, :], brow[:, :], start=False, stop=True)
                m = PE.did(last)
                V.wait(m)
                bs = slice(b * TPB, (b + 1) * TPB)
                o3 = ps.rearrange("p (c d) -> p c d", c=TPB)
                m = V.did(V.e.tensor_copy(vt[:, bs, :], o3))
                banks.done(i, m)
                v_mark = m
            SP.wait(*[x.mark() for x in parts])
            core.meet()

        wt_ring = Ring([sb(f"w_near{i}", [P, 3, P, UB * H2]) for i in range(2)])
        far_ring = Ring([sb(f"w_far{i}", [P, 2, P]) for i in range(2)])
        qp_ring = Ring([sb(f"qp{i}", [KS, H2, P], BF16) for i in range(2)])
        kp_ring = Ring([sb(f"kp{i}", [KS, H2 // 2, S], BF16) for i in range(2)])
        qr_ring = Ring([sb(f"qr{i}", [P, HG, ROW]) for i in range(3)])
        sh_bufs = [sb(f"shifted{i}", [P, HG, S]) for i in range(3)]
        sh_ring, sh_zeros = Ring(sh_bufs), [None] * len(sh_bufs)
        sc_ring = Ring([sb(f"sc{i}", [P, HG, S]) for i in range(2)])
        mx_ring = Ring([sb(f"mx{i}", [P, 2, HG]) for i in range(4)])
        sum_ring = Ring([sb(f"sums{i}", [P, 2, UB, H2]) for i in range(2)])
        half_a, half_b = (x[:, :].rearrange("p (j t) -> p j t", j=2) for x in core.sq_ring.buffers)
        o_tok = half_a[:, 0, :].rearrange("p (b t) -> p b t", b=UB)
        o_back = half_a[:, 1, :].rearrange("p (d h) -> p d h", d=D2)
        o_T = half_b
        o_rel = sb("o_rel", [NR * D2, P // NR // 2, P])
        oT_ring = Ring([sb(f"o_heads{i}", [D2, 2 * HG, P]) for i in range(2)])
        vf_ring = Ring([sb(f"v_far{i}", [P, 2, P]) for i in range(2)])
        qp_loads = [Loads(nc, f"qp_loads{i}") for i in range(2)]
        kp_loads = [Loads(nc, f"kp_loads{i}") for i in range(2)]
        qr_stores = [Loads(nc, f"qr_stores{i}") for i in range(3)]
        sh_loads = [Loads(nc, f"shift_loads{i}") for i in range(3)]
        ov_store, ov_load = Loads(nc, "rel_values_store"), Loads(nc, "rel_values_load")
        PE.wait(rk_mark, v_mark, tv_mark)

        groups = H2 // HG
        per_unit = UB * groups
        units = [(it, bp) for it in range(TPB) for bp in range(B // UB)]
        seq = [(u, bi, g) for u in range(len(units)) for bi in range(UB) for g in range(groups)]
        state = {}
        near_of = [[j for j in (it - 1, it, it + 1) if 0 <= j < TPB] for it in range(TPB)]
        far_of = [[j for j in range(TPB) if j not in near_of[it]] for it in range(TPB)]

        def place(n):
            u, bi, g = seq[n]
            it, bp = units[u]
            return u, it, bp * UB + bi, bi, g, near_of[it], far_of[it]

        def operands(n):
            u, it, b, bi, g, near, far = place(n)
            if g == 0:
                qi, qp = qp_ring.take(SP)
                at = b * S + it * P
                for r in range(3):
                    mark = qp_loads[qi].start(SP, qp[r * 3 * D2:(r + 1) * 3 * D2, :, :],
                                              q_dram.rearrange("h r d t -> (r d) h t")[:, :, at:at + P])
                state["q", u, b] = (qi, qp, mark)
            half = g // (groups // 2)
            if g % (groups // 2) == 0:
                ki, kp = kp_ring.take(SP)
                hs = slice(half * H2 // 2, (half + 1) * H2 // 2)
                for r in range(len(SPLITS)):
                    mark = kp_loads[ki].start(SP, kp[r * D2:(r + 1) * D2, :, :],
                                              k_dram[:, r // 3].rearrange("h d t -> d h t")[:, hs, b * S:(b + 1) * S])
                state["k", u, b, half] = (ki, kp, mark)

        def positions(n):
            u, it, b, bi, g, near, far = place(n)
            lo, width = (near[0] - it + 1) * P, (len(near) + 1) * P
            _, qp, mark = state["q", u, b]
            ri, qr = qr_ring.take(A)
            PE.wait(mark)
            for e in range(HG):
                i, ps = banks.take(PE)
                m = PE.did(PE.e.matmul(ps[:, 0:width], qp[:, g * HG + e, :], rk[:, lo:lo + width], start=True, stop=True))
                A.wait(m)
                m = A.did(A.e.activation(qr[:, e, 0:width], ps[:, 0:width], copy))
                banks.done(i, m)
            SP.wait(m, state["shifted", n - SLOTS][2] if n >= SLOTS else None)
            stored = qr_stores[ri].start(SP, qr_dram[n % SLOTS][:, :, 0:width].rearrange("h p t -> p h t"), qr[:, :, 0:width])
            qr_ring.done(ri, stored)
            state["stored", n] = stored

        def fetch(n):
            u, it, b, bi, g, near, far = place(n)
            si, sh = sh_ring.take(SP, G)
            if sh_zeros[si] is None or sh_zeros[si][0] != it:
                G.wait(G.last())
                G.did(G.e.memset(sh[:, :, far[0] * P:(far[-1] + 1) * P], 0.0))
                sh_zeros[si] = (it, G.last())
            SP.wait(state["stored", n])
            nk = len(near) * P
            src = bass.AP(qr_dram.tensor, n % SLOTS * HG * P * ROW + P - 1, [[ROW - 1, P], [P * ROW, HG], [1, nk]])
            state["shifted", n] = (si, sh, sh_loads[si].start(SP, sh[:, :, near[0] * P:near[0] * P + nk], src))

        def scores(n):
            u, it, b, bi, g, near, far = place(n)
            if n % per_unit == 0:
                state["sums", u] = sum_ring.take(A)
            half = g // (groups // 2)
            ki, kp, mark = state["k", u, b, half]
            qi, qp, _ = state["q", u, b]
            si, sh, sh_mark = state["shifted", n]
            ci, sc = sc_ring.take(V, A)
            xi, mx = mx_ring.take(V)
            PE.wait(mark)
            for e in range(HG):
                h = g * HG + e
                i, ps = banks.take(PE)
                last = PE.e.matmul(ps, qp[:, h, :], kp[:, h % (H2 // 2), :], start=True, stop=False)
                for j in far:
                    edge = 0 if j < it else ROW - 1
                    last = PE.e.matmul(ps[:, j * P:(j + 1) * P], qp[:, h, :], rk[:, edge:edge + 1].to_broadcast([KS, P]),
                                       start=False, stop=(j == far[-1]))
                mp = PE.did(last)
                V.wait(mp, sh_mark, sh_zeros[si][1])
                m = V.did(V.e.tensor_tensor(sc[:, e, :], ps, sh[:, e, :], ALU.add))
                banks.done(i, m)
            sh_ring.done(si, m)
            if g % (groups // 2) == groups // 2 - 1:
                kp_ring.done(ki, mp)
            if g == groups - 1:
                qp_ring.done(qi, mp)
            V.wait(m)
            m = V.did(V.e.tensor_reduce(mx[:, 0, :], sc[:, :, :], AX, ALU.max))
            V.wait(m)
            m = V.did(V.e.tensor_scalar(mx[:, 1, :], mx[:, 0, :], -isq, None, ALU.mult))
            state["sc", n] = (ci, sc, xi, mx, m)

        def exponentials(n):
            u, it, b, bi, g, near, far = place(n)
            ci, sc, xi, mx, m = state["sc", n]
            sums = state["sums", u][1]
            A.wait(m)
            for e in range(HG):
                h = g * HG + e
                m = A.did(A.e.activation(sc[:, e, :], sc[:, e, :], ACT.Exp, bias=mx[:, 1, e:e + 1], scale=isq, accum_out=sums[:, 0, bi, h:h + 1]))
            mx_ring.done(xi, m)
            state["e", n] = m

        def weights_by_key(n):
            u, it, b, bi, g, near, far = place(n)
            ci, sc = state["sc", n][:2]
            if n % per_unit == 0:
                state["wt", u] = wt_ring.take(V, A)
            wt = state["wt", u][1]
            PE.wait(state["e", n])
            turned = []
            for e in range(HG):
                h = g * HG + e
                i, ps = banks.take(PE)
                for j in range(TPB):
                    last = PE.e.transpose(ps[:, j * P:(j + 1) * P], sc[:, e, j * P:(j + 1) * P], ident[:, :])
                mt = PE.did(last)
                eng, cp = (A, lambda o, x: A.e.activation(o, x, copy)) if e % 2 else (V, lambda o, x: V.e.tensor_copy(o, x))
                p3 = ps.rearrange("p (j t) -> p j t", j=TPB)
                fi, fw = far_ring.take(eng)
                eng.wait(mt)
                eng.did(cp(wt[:, near[0] - it + 1:near[-1] - it + 2, :, bi * H2 + h], p3[:, near[0]:near[-1] + 1, :]))
                m = eng.did(cp(fw[:, 0:len(far), :], p3[:, far[0]:far[-1] + 1, :]))
                banks.done(i, m)
                turned.append((fi, fw, m))
            sc_ring.done(ci, mt)
            state["turned", n] = turned

        def values(n):
            u, it, b, bi, g, near, far = place(n)
            wt = state["wt", u][1]
            if g == 0:
                fi, vf = vf_ring.take(G)
                for k, j in enumerate(far):
                    m = G.did(G.e.tensor_tensor(vf[:, k, :], vt[:, b * TPB + j, :], v_ends[:, 0 if j < it else 1, :], ALU.add))
                state["vf"] = (fi, vf, m)
            fi, vf, mark = state["vf"]
            PE.wait(mark)
            if g % 2 == 0:
                state["heads"] = banks.take(PE)
            i, ps = state["heads"]
            for e in range(HG):
                h = g * HG + e
                at = (g % 2 * HG + e) * P
                wi, fw, m = state["turned", n][e]
                PE.wait(m)
                for j in range(TPB):
                    w = wt[:, j - it + 1, :, bi * H2 + h] if j in near else fw[:, j - far[0], :]
                    val = vt[:, b * TPB + j] if j in near else vf[:, j - far[0]]
                    last = PE.e.matmul(ps[0:D2, at:at + P], val[:, h * D2:(h + 1) * D2], w, start=(j == 0), stop=(j == TPB - 1))
                m = PE.did(last)
                far_ring.done(wi, m)
            if g == groups - 1:
                vf_ring.done(fi, m)
            if g % 2:
                oi, oT = oT_ring.take(V)
                V.wait(m)
                m = V.did(V.e.tensor_copy(oT[:, :, :].rearrange("p h t -> p (h t)"), ps[0:D2, :]))
                banks.done(i, m)
                state["oT", n] = (oi, oT, m)

        def values_by_token(n):
            u, it, b, bi, g, near, far = place(n)
            if g % 2 == 0:
                return
            if n % per_unit == 1:
                state["o", u] = banks.take(PE)
            ps = state["o", u][1]
            oi, oT, m = state["oT", n]
            PE.wait(m)
            for e in range(2 * HG):
                at = bi * P + ((g - 1) * HG + e) * D2
                last = PE.e.transpose(ps[:, at:at + D2], oT[:, e, :], ident[0:D2, 0:D2])
            state["pv", u] = m = PE.did(last)
            oT_ring.done(oi, m)

        def finish(u):
            it, bp = units[u]
            near = near_of[it]
            wi, wt = state["wt", u]
            V.wait(state["pv", u])
            i, ps = state["o", u]
            tok_mark = V.did(V.e.tensor_copy(o_tok[:, :, :].rearrange("p b d -> p (b d)"), ps[:, 0:UB * P]))
            banks.done(i, tok_mark)
            blocks = P // NR
            per = 512 // P
            for part in range(blocks // per):
                half, at = divmod(part, blocks // per // 2)
                if at == 0:
                    A.wait(state.get("rel_stored"))
                i, ps = banks.take(PE)
                for k in range(per):
                    q = (part * per + k) * NR
                    for j in near:
                        v = 2 * M2 - 1 - q - (NR - 1) + (j - it) * P
                        last = PE.e.matmul(ps[0:NR * D2, k * P:(k + 1) * P], tv[:, v:v + NR, :].rearrange("p v d -> p (v d)"),
                                           wt[:, j - it + 1, q:q + NR, :].rearrange("p q b -> p (q b)"),
                                           start=(j == near[0]), stop=(j == near[-1]))
                m = PE.did(last)
                A.wait(m)
                m = A.did(A.e.activation(o_rel[:, at * per:(at + 1) * per, :].rearrange("p k c -> p (k c)"), ps[0:NR * D2, :], copy))
                banks.done(i, m)
                if (part + 1) % (blocks // per // 2) == 0:
                    SP.wait(m)
                    for r in range(NR):
                        own = slice((NR - 1 - r) * D2, (NR - r) * D2)
                        stored = ov_store.start(SP, o_dram[u, :, half * blocks // 2:(half + 1) * blocks // 2, r, :],
                                                o_rel[own, :, r * UB * H2:(r + 1) * UB * H2])
                    state["rel_stored"] = stored
                yield
            wt_ring.done(wi, PE.last())
            yield
            SP.wait(stored, state.get("back_free"))
            back = ov_load.start(SP, o_back[:, :, :], o_dram[u].rearrange("d n r b -> (n r) d b"))
            yield
            yield
            si, sums = state["sums", u]
            V.wait(state["e", (u + 1) * per_unit - 1])
            m = V.did(V.e.reciprocal(sums[:, 1], sums[:, 0]))
            V.wait(back, m, tok_mark)
            o4 = o_tok[:, :, :].rearrange("p b (h d) -> p (b h) d", d=D2)
            m = V.did(V.e.tensor_tensor(o4, o4, o_back[:, :, :].rearrange("p d h -> p h d"), ALU.add))
            state["back_free"] = m
            V.wait(m)
            m = V.did(V.e.tensor_tensor(o4, o4, sums[:, 1].rearrange("p b h -> p (b h)").unsqueeze(2).to_broadcast([P, UB * H2, D2]), ALU.mult))
            sum_ring.done(si, m)
            yield
            i, ps = banks.take(PE)
            PE.wait(m)
            for b in range(UB):
                last = PE.e.transpose(ps[:, b * P:(b + 1) * P], o_tok[:, b, :], ident[:, :])
            m = PE.did(last)
            V.wait(m)
            m = V.did(V.e.tensor_copy(o_T[:, 0, :], ps[:, 0:UB * P]))
            banks.done(i, m)
            yield
            i, ps = banks.take(PE)
            PE.wait(m)
            m = PE.did(PE.e.matmul(ps[:, 0:UB * P], woT[:, :], o_T[:, 0, :], start=True, stop=True))
            V.wait(m)
            m = V.did(V.e.tensor_scalar(o_T[:, 1, :], ps[:, 0:UB * P], colb[:, 2:3], None, ALU.add))
            banks.done(i, m)
            V.wait(m)
            for b in range(UB):
                x = xT[:, bp * UB + b, it * P:(it + 1) * P]
                V.did(V.e.scalar_tensor_tensor(out=x, in0=o_T[:, 1, b * P:(b + 1) * P], scalar=gate[:, 1, 0, bp * UB + b:bp * UB + b + 1],
                                               in1=x, op0=ALU.mult, op1=ALU.add))
            yield

        operands(0)
        ends = []
        last_lag = 5
        for n in range(len(seq) + last_lag):
            for stage, lag in ((fetch, 1), (weights_by_key, 4), (scores, 3), (positions, 0), (values_by_token, last_lag),
                               (values, 4), (exponentials, 3)):
                if 0 <= n - lag < len(seq):
                    stage(n - lag)
            if n + 1 < len(seq):
                operands(n + 1)
            ends = [e for e in ends if next(e, "done") is None]
            done = n - last_lag
            if done >= 0 and done % per_unit == per_unit - 1:
                ends.append(finish(done // per_unit))
        for e in ends:
            for _ in e:
                pass
        for s in (*qr_stores, ov_store, *parts, ext):
            SP.wait(s.mark())


def experts(core):
    nc, io, PE, V, A, G, SP, banks = core.nc, core.io, core.PE, core.V, core.A, core.G, core.SP, core.banks
    ident, identb, xT, modT, gate, psum = core.ident, core.identb, core.xT, core.modT, core.gate, core.psum
    NJ = HD // P
    with ExitStack() as scope:
        def sb(name, shape, dt=F32):
            return core.sbuf(scope, name, shape, dt)

        hT, xc = sb("hT3", [P, B, S]), sb("xc3", [P, B, S])
        rw, rwT = sb("router", [NE, P]), sb("routerT", [P, NE])
        order = sb("order", [P, NE])
        logits, pick = sb("logits", [P, NT, NE]), sb("pick", [P, NT, NE])
        best = sb("best", [P, 2, NT])
        chosen = sb("chosen", [P, NT, NE], BF16)
        fc_ring = Ring([sb(f"fc{i}", [P, HD]) for i in range(3)])
        pr_ring = Ring([sb(f"pr{i}", [P, HD]) for i in range(3)])
        h_parts = [sb(f"h_part{i}", [P, B, S], F32R) for i in range(2)]
        fc_parts = Ring([sb(f"fc_parts{i}", [P, 2, HD], F32R) for i in range(2)])
        pT_ring = Ring([sb(f"prT{i}", [P, 2, NJ, P], F32R) for i in range(2)])
        xe_ring = Ring([sb(f"xe{i}", [P, 2, S], F32R) for i in range(3)])
        r_ring = Ring([sb(f"relu{i}", [P, S]) for i in range(3)])
        s_ring = Ring([sb(f"square{i}", [P, S]) for i in range(3)])
        sp_ring = Ring([sb(f"square_parts{i}", [P, 2, S], F32R) for i in range(5)])
        loads = Loads(nc, "router_load")
        loads.start(SP, rw[:, :], io["L1_ffn_router_w"])
        loads.start(SP, order[:, :], io["c_first"])
        w_loads = [Loads(nc, f"expert_loads{i}") for i in range(3)]
        w_marks = {}

        def load(e, *free):
            fi, fc = fc_ring.take(SP)
            ri, pr = pr_ring.take(SP)
            w_loads[e % 3].start(SP, fc[:, :], io["L1_ffn_expert_fc"][e])
            w_marks[e] = (fi, fc, ri, pr, w_loads[e % 3].start(SP, pr[:, :], io["L1_ffn_expert_proj"][e]))

        for e in range(2):
            load(e)
        h_marks = core.side_by_side([core.layer_norm_steps(hT[:, b, :], xT[:, b, :], xc[:, b, :], modT[:, 1, 4, b:b + 1],
                                                           modT[:, 1, 3, b:b + 1], b) for b in range(B)])
        m = V.did(V.e.tensor_copy(identb[:, :], ident[:, :]))
        PE.wait(m, loads.mark())
        i, ps = banks.take(PE)
        m = PE.did(PE.e.transpose(ps[:, 0:NE], rw[:, :], ident[0:NE, 0:NE]))
        V.wait(m, loads.mark())
        m = V.did(V.e.tensor_copy(rwT[:, :], ps[:, 0:NE]))
        banks.done(i, m)
        PE.wait(m)
        i, ps = banks.take(PE)
        PE.wait(*h_marks)
        for t in range(NT):
            b, c = divmod(t, TPB)
            last = PE.e.matmul(ps[:, t * NE:(t + 1) * NE], hT[:, b, c * P:(c + 1) * P], rwT[:, :], start=True, stop=True)
        m = PE.did(last)
        V.wait(m)
        m = V.did(V.e.tensor_copy(logits[:, :, :].rearrange("p t e -> p (t e)"), ps[:, 0:NT * NE]))
        banks.done(i, m)
        wide = lambda j: best[:, j, :].unsqueeze(2).to_broadcast([P, NT, NE])
        V.wait(m)
        m = V.did(V.e.tensor_reduce(best[:, 0, :], logits[:, :, :], AX, ALU.max))
        V.wait(m)
        m = V.did(V.e.tensor_tensor(pick[:, :, :], logits[:, :, :], wide(0), ALU.is_ge))
        V.wait(m)
        m = V.did(V.e.tensor_tensor(pick[:, :, :], pick[:, :, :], order[:, :].unsqueeze(1).to_broadcast([P, NT, NE]), ALU.mult))
        V.wait(m)
        m = V.did(V.e.tensor_reduce(best[:, 1, :], pick[:, :, :], AX, ALU.max))
        V.wait(m)
        m = V.did(V.e.tensor_tensor(chosen[:, :, :], pick[:, :, :], wide(1), ALU.is_equal))
        chosen_mark = m

        for b in range(B):
            A.wait(h_marks[b])
            m = A.did(A.e.activation(h_parts[0][:, b, :], hT[:, b, :], ACT.Copy))
            V.wait(m)
            V.did(V.e.tensor_tensor(h_parts[1][:, b, :], hT[:, b, :], h_parts[0][:, b, :].bitcast(F32), ALU.subtract))
        V.wait(V.last())

        def product(out, w, x, first, last):
            PE.e.matmul(out, w[0], x[1], start=first, stop=False)
            PE.e.matmul(out, w[1], x[0], start=False, stop=False)
            return PE.did(PE.e.matmul(out, w[0], x[0], start=False, stop=last))

        work = [(e, b) for e in range(NE) for b in range(B)]
        core.meet()
        small = Ring([psum[:, i, :] for i in range(4)])
        sums = [psum[:, 4 + b, :] for b in range(B)]
        masked, turned, fcs = {}, {}, {}

        def prepare(n):
            e, b = work[n]
            if b == 0:
                if 1 <= e < NE - 1:
                    load(e + 1)
                fi, fc, ri, pr, mark = w_marks[e]
                fpi, fp = fc_parts.take(A)
                A.wait(mark)
                m = A.did(A.e.activation(fp[:, 0, :], fc[:, :], ACT.Copy))
                G.wait(m)
                m = G.did(G.e.tensor_tensor(fp[:, 1, :], fc[:, :], fp[:, 0, :].bitcast(F32), ALU.subtract))
                fc_ring.done(fi, m)
                fcs[e] = (fpi, fp, m)
                i, ps = small.take(PE)
                PE.wait(mark)
                for j in range(NJ):
                    last = PE.e.transpose(ps[:, j * P:(j + 1) * P], pr[:, j * P:(j + 1) * P], ident[:, :])
                m = PE.did(last)
                pr_ring.done(ri, m)
                ti, pT = pT_ring.take(A, V)
                high, low = (pT[:, k, :, :].rearrange("p j d -> p (j d)") for k in range(2))
                A.wait(m)
                m = A.did(A.e.activation(high, ps, ACT.Copy))
                V.wait(m)
                m = V.did(V.e.tensor_tensor(low, ps, high.bitcast(F32), ALU.subtract))
                small.done(i, m)
                turned[e] = (ti, pT, m)
            i, ps = small.take(PE)
            PE.wait(chosen_mark)
            for c in range(TPB):
                last = PE.e.matmul(ps[:, c * P:(c + 1) * P], chosen[:, b * TPB + c, e:e + 1].to_broadcast([P, P]), identb[:, :], start=True, stop=True)
            m = PE.did(last)
            xi, xe = xe_ring.take(V)
            V.wait(m)
            for k in range(2):
                m = V.did(V.e.tensor_tensor(xe[:, k, :], h_parts[k][:, b, :].bitcast(F32), ps, ALU.mult))
            small.done(i, m)
            masked[n] = (xi, xe, m)

        hidden = {}

        def up(n, j):
            e, b = work[n]
            fi, fp, f_mark = fcs[e]
            xi, xe, mark = masked[n]
            i, ps = small.take(PE)
            PE.wait(mark, f_mark)
            m = product(ps, [fp[:, k, j * P:(j + 1) * P] for k in range(2)], [xe[:, k, :] for k in range(2)], True, True)
            if j == NJ - 1:
                xe_ring.done(xi, m)
                if b == B - 1:
                    fc_parts.done(fi, m)
            ri, r = r_ring.take(V)
            V.wait(m)
            m = V.did(V.e.tensor_scalar(r[:, :], ps, 0.0, None, ALU.max))
            small.done(i, m)
            si, s = s_ring.take(A)
            A.wait(m)
            m = A.did(A.e.activation(s[:, :], r[:, :], ACT.Square))
            r_ring.done(ri, m)
            pi, parts = sp_ring.take(A, G)
            A.wait(m)
            m = A.did(A.e.activation(parts[:, 0, :], s[:, :], ACT.Copy))
            G.wait(m)
            m = G.did(G.e.tensor_tensor(parts[:, 1, :], s[:, :], parts[:, 0, :].bitcast(F32), ALU.subtract))
            s_ring.done(si, m)
            hidden[n, j] = (pi, parts, m)

        def down(n, j):
            e, b = work[n]
            ti, pT, mark = turned[e]
            si, s, m = hidden[n, j]
            PE.wait(mark, m)
            m = product(sums[b], [pT[:, k, j, :] for k in range(2)], [s[:, k, :] for k in range(2)],
                        e == 0 and j == 0, e == NE - 1 and j == NJ - 1)
            sp_ring.done(si, m)
            if b == B - 1 and j == NJ - 1:
                pT_ring.done(ti, m)
            return m

        steps = [(n, j) for n in range(len(work)) for j in range(NJ)]
        prepare(0)
        lag = 4
        for k in range(len(steps) + lag):
            if k < len(steps):
                n, j = steps[k]
                if j == 1 and n + 1 < len(work):
                    prepare(n + 1)
                up(n, j)
            if k >= lag:
                m = down(*steps[k - lag])
        V.wait(m)
        for b in range(B):
            V.did(V.e.scalar_tensor_tensor(out=xT[:, b, :], in0=sums[b], scalar=gate[:, 1, 1, b:b + 1], in1=xT[:, b, :], op0=ALU.mult, op1=ALU.add))
        core.meet()


def constants():
    f = np.float32
    half = np.arange(0, DH, 2, dtype=f)
    inv_freq = (f(1.0) / f(10000.0) ** (half / f(DH))).astype(f)
    pos = np.arange(S, dtype=f)
    freqs = np.concatenate([pos[:, None] * inv_freq[None, :]] * 2, -1)
    power = (pos - S // 2) / f(WIN // 2)
    scale = ((half + f(0.4 * DH)) / f(1.4 * DH))[None, :] ** power[:, None]
    scale = np.concatenate([scale, scale], -1).astype(np.float64)
    sign = np.where(np.arange(DH) < DH // 2, -1.0, 1.0)
    cos, sin = np.cos(freqs.astype(np.float64)), np.sin(freqs.astype(np.float64)) * sign
    rot = np.stack([8.0 * cos * scale, 8.0 * sin * scale, cos / scale, sin / scale])
    rot = rot.reshape(4, TPB, P, DH).transpose(2, 0, 1, 3)
    i, j = np.arange(QB)[:, None], np.arange(KB)[None, :] - WIN
    ok = (j <= i) & (j >= i - WIN)
    mask = np.stack([ok, ok & (j >= 0)], 1)
    mask = np.where(np.concatenate([mask, mask]), 0.0, MASKED)
    up = np.triu(np.ones((P, P)), 1) * ETA
    eye = np.eye(P)
    out = {
        "c_ident": eye, "c_center": eye - 1.0 / P, "c_lower": up.T,
        "c_upper": np.stack([up, -(up + eye * ETA)], 1), "c_rot": rot, "c_mask": mask,
        "c_first": np.broadcast_to(NE - np.arange(NE), (P, NE)),
    }
    return {n: np.ascontiguousarray(a, dtype=f) for n, a in out.items()}


def kernel(**inputs):
    import concourse.bacc as bacc
    from concourse.bass_utils import run_bass_kernel_spmd

    nc = bacc.Bacc("TRN2", target_bir_lowering=False, num_devices=1)
    arrays = {n: np.ascontiguousarray(a) for n, a in inputs.items()}
    arrays.update(constants())
    io = {n: nc.dram_tensor(n, a.shape, mybir.dt.from_np(a.dtype), kind="ExternalInput").ap() for n, a in arrays.items()}
    io["out"] = nc.dram_tensor("out", (B, S, P), F32, kind="ExternalOutput").ap()
    build(nc, io)
    result = run_bass_kernel_spmd(nc, [arrays], core_ids=[0])
    return result.results[0]["out"]
```
